# Optimizing a Trainium2 kernel written in Bass

```python
import numpy as np
import jax
import jax.numpy as jnp

def _softmax(x, axis=-1):
    return jax.nn.softmax(x, axis=axis)

def _gelu(x):
    return jax.nn.gelu(x, approximate=True)

def _silu(x):
    return jax.nn.silu(x)

def _sigmoid(x):
    return jax.nn.sigmoid(x)

def _layernorm(x, axis=-1, eps=1e-05):
    m = jnp.mean(x, axis=axis, keepdims=True)
    v = jnp.var(x, axis=axis, keepdims=True)
    return (x - m) / jnp.sqrt(v + eps)

def _scatter_add(tgt, idx, src, axis=0):
    return tgt.at[idx].add(src)

def _segment_sum(src, seg, n):
    return jax.ops.segment_sum(src, seg, n)
kernel_name = 'mk_perceiver_d4_seqx_r8_ae1d11'

def setup_inputs(seed: int=0):
    np.random.seed(seed)
    _w = jnp.asarray

    def _rec_inputs():
        import jax
        import jax.numpy as jnp
        _rk = jax.random.key(seed)
        x = 7.22e-05 + 1 * jax.random.normal(jax.random.fold_in(_rk, 1), (32, 32, 256), jnp.float32)
        _lenS = 32 - jax.random.randint(jax.random.fold_in(_rk, 7), (32,), 0, max(1, 32 // 4) + 1, jnp.int32)
        _lenS2 = 257 - jax.random.randint(jax.random.fold_in(_rk, 8), (32,), 0, max(1, 257 // 4) + 1, jnp.int32)
        _ctx_512P = jax.random.normal(jax.random.fold_in(_rk, 11), (32, 16, 64), jnp.float32)
        _ctx_512c = jax.random.dirichlet(jax.random.fold_in(_rk, 511), 0.3 * jnp.ones((16,), jnp.float32), (32, 257))
        _ctx_512t = jnp.einsum('bsk,bkd->bsd', _ctx_512c, _ctx_512P)
        _ctx_512t = _ctx_512t * jax.lax.rsqrt(jnp.mean(jnp.square(_ctx_512t)) + 1e-12) * 0.953939
        ctx_512 = -0.000514642 + 1.00011 * (_ctx_512t + 0.3 * jax.random.normal(jax.random.fold_in(_rk, 611), (32, 257, 64), jnp.float32))
        return (x, ctx_512)
    x, ctx_512 = _rec_inputs()

    def _L0_xattn_setup():
        import jax, jax.numpy as jnp
        import numpy as np
        B, S, H, NH, L = (2, 256, 256, 16, 64)
        HD = H // NH
        key = jax.random.key(seed)
        k1, k2, k3, k4, k5 = jax.random.split(key, 5)
        scale = 0.02
        return {'q': jax.random.normal(k1, (B, S, H), dtype=jnp.float32), 'latent_kv': jax.random.normal(k2, (B, S, L), dtype=jnp.float32), 'Wq': jax.random.normal(k3, (H, H), dtype=jnp.float32) * scale, 'Wkv_expand': jax.random.normal(k4, (2 * H, L), dtype=jnp.float32) * scale, 'Wout': jax.random.normal(k5, (H, H), dtype=jnp.float32) * scale}
    _L0_xattn_all = _L0_xattn_setup()
    _L0_xattn_in = {k: v for k, v in _L0_xattn_all.items() if k in ('Wq', 'Wkv_expand', 'Wout')}
    del _L0_xattn_all

    def _L0_attn_setup():
        import jax, jax.numpy as jnp
        import numpy as np
        C = 8.0

        def _linear_scan(alpha, xbeta):

            def combine(e1, e2):
                a1, b1 = e1
                a2, b2 = e2
                return (a2 * a1, a2 * b1 + b2)
            _, h = jax.lax.associative_scan(combine, (alpha, xbeta), axis=1)
            return h
        dim = 256
        B, T = (4, 512)
        key = jax.random.key(seed)
        k_x, k_wi, k_wg = jax.random.split(key, 3)
        std = dim ** (-0.5)
        x = jax.random.normal(k_x, (B, T, dim), dtype=jnp.float32)
        W_in = jax.random.normal(k_wi, (dim, dim), dtype=jnp.float32) * std
        b_in = jnp.zeros((dim,), dtype=jnp.float32)
        W_gate = jax.random.normal(k_wg, (dim, dim), dtype=jnp.float32) * std
        b_gate = jnp.zeros((dim,), dtype=jnp.float32)
        forget_lambda = jnp.linspace(-4.323, -9.0, dim, dtype=jnp.float32)
        return {'x': x, 'W_in': W_in, 'b_in': b_in, 'W_gate': W_gate, 'b_gate': b_gate, 'forget_lambda': forget_lambda}
    _L0_attn_all = _L0_attn_setup()
    _L0_attn_in = {k: v for k, v in _L0_attn_all.items() if k in ('W_in', 'b_in', 'W_gate', 'b_gate', 'forget_lambda')}
    del _L0_attn_all

    def _L0_ffn_setup():
        import jax, jax.numpy as jnp
        import numpy as np
        HIDDEN = 256
        INTER = 1024
        SCALE = 64.0

        def fwht(x):
            orig_shape = x.shape
            n = orig_shape[-1]
            x = x.reshape(-1, n)
            h = 1
            while h < n:
                x = x.reshape(-1, n // (2 * h), 2, h)
                a, b = (x[:, :, 0, :], x[:, :, 1, :])
                x = jnp.stack([a + b, a - b], axis=2).reshape(-1, n)
                h *= 2
            return (x / jnp.sqrt(jnp.asarray(n, x.dtype))).reshape(orig_shape)
        key = jax.random.key(seed)
        ks = jax.random.split(key, 8)
        inp = jax.random.normal(ks[0], (4, 256, HIDDEN), dtype=jnp.float32)
        SU_ug = jnp.where(jax.random.bernoulli(ks[1], 0.5, (HIDDEN,)), 1.0, -1.0).astype(jnp.float32)
        SU_dp = jnp.where(jax.random.bernoulli(ks[2], 0.5, (INTER,)), 1.0, -1.0).astype(jnp.float32)
        Wscale_ug = jax.random.uniform(ks[3], (2 * INTER,), jnp.float32, 0.5, 1.5)
        Wscale_dp = jax.random.uniform(ks[4], (HIDDEN,), jnp.float32, 0.5, 1.5)
        W_up = jax.random.normal(ks[5], (INTER, HIDDEN), dtype=jnp.float32) * 0.02
        W_gate = jax.random.normal(ks[6], (INTER, HIDDEN), dtype=jnp.float32) * 0.02
        W_down = jax.random.normal(ks[7], (HIDDEN, INTER), dtype=jnp.float32) * 0.02
        return {'input': inp, 'SU_ug': SU_ug, 'SU_dp': SU_dp, 'Wscale_ug': Wscale_ug, 'Wscale_dp': Wscale_dp, 'W_up': W_up, 'W_gate': W_gate, 'W_down': W_down}
    _L0_ffn_all = _L0_ffn_setup()
    _L0_ffn_in = {k: v for k, v in _L0_ffn_all.items() if k in ('SU_ug', 'SU_dp', 'Wscale_ug', 'Wscale_dp', 'W_up', 'W_gate', 'W_down')}
    del _L0_ffn_all

    def _L1_xattn_setup():
        import jax, jax.numpy as jnp
        import numpy as np
        B, S, L = (2, 128, 128)
        DIM_Q, H, K, D_C, D_CQ, R = (256, 16, 128, 64, 192, 64)

        def _rope_tables(length, dim):
            inv = 1.0 / 10000.0 ** (jnp.arange(0, dim, 2, dtype=jnp.float32) / dim)
            f = jnp.arange(length, dtype=jnp.float32)[:, None] * inv[None, :]
            sin = jnp.repeat(jnp.sin(f), 2, axis=-1)
            cos = jnp.repeat(jnp.cos(f), 2, axis=-1)
            return (sin, cos)

        def _rotate_half(x):
            half = x.shape[-1] // 2
            return jnp.concatenate([-x[..., half:], x[..., :half]], axis=-1)

        def _apply_rope(x, sin, cos):
            return x * cos + _rotate_half(x) * sin
        key = jax.random.key(seed)
        ks = jax.random.split(key, 8)
        return {'hidden_q': jax.random.normal(ks[0], (B, S, DIM_Q), jnp.float32), 'kv_c': jax.random.normal(ks[1], (B, L, D_C), jnp.float32), 'Wq': jax.random.normal(ks[2], (H * K, DIM_Q), jnp.float32) / np.sqrt(DIM_Q).astype(np.float32), 'w_kc_q': jax.random.normal(ks[3], (H, K, D_CQ), jnp.float32) / np.sqrt(K).astype(np.float32), 'w_kc_kv': jax.random.normal(ks[4], (H, K, D_C), jnp.float32) / np.sqrt(K).astype(np.float32), 'W_qr': jax.random.normal(ks[5], (H, D_CQ, R), jnp.float32) / np.float32(np.sqrt(D_CQ) * np.sqrt(R)), 'W_kr': jax.random.normal(ks[6], (H, D_C, R), jnp.float32) / np.sqrt(D_C).astype(np.float32), 'Wo': jax.random.normal(ks[7], (DIM_Q, H * K), jnp.float32) / np.sqrt(H * K).astype(np.float32)}
    _L1_xattn_all = _L1_xattn_setup()
    _L1_xattn_in = {k: v for k, v in _L1_xattn_all.items() if k in ('Wq', 'w_kc_q', 'w_kc_kv', 'W_qr', 'W_kr', 'Wo')}
    del _L1_xattn_all

    def _L1_attn_setup():
        import jax, jax.numpy as jnp
        import numpy as np
        import math
        D = 256
        K = 64
        NUM_HEADS = 32
        HEAD_DIM = K // NUM_HEADS
        SPARSITY = 0.1
        LN_EPS = 1e-05
        key = jax.random.key(seed)
        ks = jax.random.split(key, 12)
        B, S = (1, 128)
        sc = 0.02
        inp = {'x': jax.random.normal(ks[0], (B, S, D), dtype=jnp.float32), 'gamma': jnp.ones((D,), jnp.float32), 'beta': jnp.zeros((D,), jnp.float32), 'W1': jax.random.normal(ks[1], (128, D), jnp.float32) * sc, 'b1': jnp.zeros((128,), jnp.float32), 'W2': jax.random.normal(ks[2], (64, 128), jnp.float32) * sc, 'b2': jnp.zeros((64,), jnp.float32), 'W3': jax.random.normal(ks[3], (1, 64), jnp.float32) * sc, 'b3': jnp.zeros((1,), jnp.float32), 'Wqkv': jax.random.normal(ks[4], (3 * K, D), jnp.float32) * sc, 'bqkv': jnp.zeros((3 * K,), jnp.float32), 'Wout': jax.random.normal(ks[5], (D, K), jnp.float32) * sc, 'bout': jnp.zeros((D,), jnp.float32)}
        return inp
    _L1_attn_all = _L1_attn_setup()
    _L1_attn_in = {k: v for k, v in _L1_attn_all.items() if k in ('gamma', 'beta', 'W1', 'b1', 'W2', 'b2', 'W3', 'b3', 'Wqkv', 'bqkv', 'Wout', 'bout')}
    del _L1_attn_all

    def _L1_ffn_setup():
        import jax, jax.numpy as jnp
        import numpy as np
        TOP_P = 0.9
        S, B, H, I, E = (256, 4, 256, 512, 8)

        def _top_p_weights(probs, top_p):
            order = jnp.argsort(-probs, axis=-1)
            sp = jnp.take_along_axis(probs, order, axis=-1)
            cum = jnp.cumsum(sp, axis=-1)
            exceed = cum > top_p
            first_idx = jnp.argmax(exceed, axis=-1)
            first = jnp.arange(probs.shape[-1])[None, :] == first_idx[:, None]
            keep = ~exceed | first
            kept = jnp.where(keep, sp, 0.0)
            t_idx = jnp.arange(probs.shape[0])[:, None]
            return jnp.zeros_like(probs).at[t_idx, order].set(kept)
        key = jax.random.key(seed)
        ks = jax.random.split(key, 5)
        scale = 0.02
        return {'hidden_states': jax.random.normal(ks[0], (S, B, H), dtype=jnp.float32), 'router_w': jax.random.normal(ks[1], (E, H), dtype=jnp.float32) * scale, 'gate_w': jax.random.normal(ks[2], (E, I, H), dtype=jnp.float32) * scale, 'up_w': jax.random.normal(ks[3], (E, I, H), dtype=jnp.float32) * scale, 'down_w': jax.random.normal(ks[4], (E, H, I), dtype=jnp.float32) * scale}
    _L1_ffn_all = _L1_ffn_setup()
    _L1_ffn_in = {k: v for k, v in _L1_ffn_all.items() if k in ('router_w', 'gate_w', 'up_w', 'down_w')}
    del _L1_ffn_all

    def _L2_xattn_setup():
        import jax, jax.numpy as jnp
        import numpy as np
        B, S, H, NH, L = (2, 256, 256, 16, 64)
        HD = H // NH
        key = jax.random.key(seed)
        k1, k2, k3, k4, k5 = jax.random.split(key, 5)
        scale = 0.02
        return {'q': jax.random.normal(k1, (B, S, H), dtype=jnp.float32), 'latent_kv': jax.random.normal(k2, (B, S, L), dtype=jnp.float32), 'Wq': jax.random.normal(k3, (H, H), dtype=jnp.float32) * scale, 'Wkv_expand': jax.random.normal(k4, (2 * H, L), dtype=jnp.float32) * scale, 'Wout': jax.random.normal(k5, (H, H), dtype=jnp.float32) * scale}
    _L2_xattn_all = _L2_xattn_setup()
    _L2_xattn_in = {k: v for k, v in _L2_xattn_all.items() if k in ('Wq', 'Wkv_expand', 'Wout')}
    del _L2_xattn_all

    def _L2_attn_setup():
        import jax, jax.numpy as jnp
        import numpy as np
        DIM = 256
        HIDDEN = 256
        HEADS = 4
        HD = HIDDEN // HEADS
        EPS = 1e-06
        BATCH = 4
        SEQ = 256
        key = jax.random.key(seed)
        k0, k1, k2, k3 = jax.random.split(key, 4)
        s = 0.02
        x = jax.random.normal(k0, (BATCH, SEQ, DIM), dtype=jnp.float32)
        W_in = jax.random.normal(k1, (HIDDEN, DIM), dtype=jnp.float32) * s
        W_gate = jax.random.normal(k2, (4 * HIDDEN, HIDDEN), dtype=jnp.float32) * s
        b_gate = jnp.zeros((4 * HIDDEN,), dtype=jnp.float32)
        rms_w = jnp.ones((HD,), dtype=jnp.float32)
        W_out = jax.random.normal(k3, (DIM, HIDDEN), dtype=jnp.float32) * s
        return {'x': x, 'W_in': W_in, 'W_gate': W_gate, 'b_gate': b_gate, 'rms_w': rms_w, 'W_out': W_out}
    _L2_attn_all = _L2_attn_setup()
    _L2_attn_in = {k: v for k, v in _L2_attn_all.items() if k in ('W_in', 'W_gate', 'b_gate', 'rms_w', 'W_out')}
    del _L2_attn_all

    def _L2_ffn_setup():
        import jax, jax.numpy as jnp
        import numpy as np
        from jax import lax
        H = 256
        I = 176
        E = 16
        TOP_K = 6
        IS = 2 * I

        def _swiglu(x, w13_, w2_):
            gu = x @ w13_.T
            g, u = jnp.split(gu, 2, axis=-1)
            return jax.nn.silu(g) * u @ w2_.T
        key = jax.random.key(seed)
        ks = jax.random.split(key, 6)
        return {'hidden_states': jax.random.normal(ks[0], (1, 256, H), jnp.float32), 'gate_w': jax.random.normal(ks[1], (E, H), jnp.float32) * 0.02, 'w13': jax.random.normal(ks[2], (E, 2 * I, H), jnp.float32) * 0.02, 'w2': jax.random.normal(ks[3], (E, H, I), jnp.float32) * 0.02, 'sw13': jax.random.normal(ks[4], (2 * IS, H), jnp.float32) * 0.02, 'sw2': jax.random.normal(ks[5], (H, IS), jnp.float32) * 0.02}
    _L2_ffn_all = _L2_ffn_setup()
    _L2_ffn_in = {k: v for k, v in _L2_ffn_all.items() if k in ('gate_w', 'w13', 'w2', 'sw13', 'sw2')}
    del _L2_ffn_all

    def _L3_xattn_setup():
        import jax, jax.numpy as jnp
        import numpy as np
        B, S, L = (2, 128, 128)
        DIM_Q, H, K, D_C, D_CQ, R = (256, 16, 128, 64, 192, 64)

        def _rope_tables(seq_len, dim, dtype):
            inv_freq = 1.0 / 10000.0 ** (jnp.arange(0, dim, 2, dtype=dtype) / dim)
            t = jnp.arange(seq_len, dtype=dtype)
            freqs = t[:, None] * inv_freq[None, :]
            sin = jnp.repeat(jnp.sin(freqs), 2, axis=-1)
            cos = jnp.repeat(jnp.cos(freqs), 2, axis=-1)
            return (sin, cos)

        def _rotate_half(x):
            h = x.shape[-1] // 2
            return jnp.concatenate([-x[..., h:], x[..., :h]], axis=-1)
        key = jax.random.key(seed)
        ks = jax.random.split(key, 8)
        s_in = 1.0 / np.sqrt(DIM_Q)
        s_k = 1.0 / np.sqrt(K)
        s_cq = 1.0 / np.sqrt(D_CQ)
        s_c = 1.0 / np.sqrt(D_C)
        return {'hidden_q': jax.random.normal(ks[0], (B, S, DIM_Q), jnp.float32), 'kv_c': jax.random.normal(ks[1], (B, L, D_C), jnp.float32), 'Wq': jax.random.normal(ks[2], (H * K, DIM_Q), jnp.float32) * s_in, 'w_kc_q': jax.random.normal(ks[3], (H, K, D_CQ), jnp.float32) * s_k, 'w_kc_kv': jax.random.normal(ks[4], (H, K, D_C), jnp.float32) * s_k, 'W_qr': jax.random.normal(ks[5], (H, D_CQ, R), jnp.float32) * s_cq / np.sqrt(R), 'W_kr': jax.random.normal(ks[6], (H, D_C, R), jnp.float32) * s_c, 'Wo': jax.random.normal(ks[7], (DIM_Q, H * K), jnp.float32) * s_k}
    _L3_xattn_all = _L3_xattn_setup()
    _L3_xattn_in = {k: v for k, v in _L3_xattn_all.items() if k in ('Wq', 'w_kc_q', 'w_kc_kv', 'W_qr', 'W_kr', 'Wo')}
    del _L3_xattn_all

    def _L3_attn_setup():
        import jax, jax.numpy as jnp
        import numpy as np
        D_IN = 256
        D_OUT = 256
        NUM_HEADS = 16
        NUM_KV_GROUPS = 4
        GROUP_SIZE = NUM_HEADS // NUM_KV_GROUPS
        HEAD_DIM = D_OUT // NUM_HEADS
        key = jax.random.key(seed)
        ks = jax.random.split(key, 6)
        b, n = (2, 256)
        x = jax.random.normal(ks[0], (b, n, D_IN), dtype=jnp.float32)
        Wq = jax.random.normal(ks[1], (D_IN, D_OUT), dtype=jnp.float32) * (1.0 / np.sqrt(D_IN))
        Wk = jax.random.normal(ks[2], (D_IN, NUM_KV_GROUPS * HEAD_DIM), dtype=jnp.float32) * (1.0 / np.sqrt(D_IN))
        Wv = jax.random.normal(ks[3], (D_IN, NUM_KV_GROUPS * HEAD_DIM), dtype=jnp.float32) * (1.0 / np.sqrt(D_IN))
        Wo = jax.random.normal(ks[4], (D_OUT, D_OUT), dtype=jnp.float32) * (1.0 / np.sqrt(D_OUT))
        bo = jax.random.normal(ks[5], (D_OUT,), dtype=jnp.float32) * 0.01
        return {'x': x, 'Wq': Wq, 'Wk': Wk, 'Wv': Wv, 'Wo': Wo, 'bo': bo}
    _L3_attn_all = _L3_attn_setup()
    _L3_attn_in = {k: v for k, v in _L3_attn_all.items() if k in ('Wq', 'Wk', 'Wv', 'Wo', 'bo')}
    del _L3_attn_all

    def _L3_ffn_setup():
        import jax, jax.numpy as jnp
        import numpy as np
        D_MODEL = 256
        HIDDEN = 4 * D_MODEL
        EPS = 1e-05
        QB = 127.0

        def _ste(orig, quant):
            return orig + jax.lax.stop_gradient(quant - orig)

        def _act_quant(a):
            scale = QB / jnp.clip(jnp.max(jnp.abs(a), axis=-1, keepdims=True), 1e-05)
            q = jnp.clip(jnp.round(a * scale), -QB, QB) / scale
            return _ste(a, q)

        def _weight_quant(w):
            s = jnp.clip(jnp.mean(jnp.abs(w)), 1e-05)
            q = jnp.clip(jnp.round(w / s), -1.0, 1.0) * s
            return _ste(w, q)

        def _bitlinear(x, w):
            return jnp.einsum('bsd,od->bso', _act_quant(x), _weight_quant(w))

        def _rmsnorm(x, g):
            var = jnp.mean(jnp.square(x), axis=-1, keepdims=True)
            return x * jax.lax.rsqrt(var + EPS) * g
        key = jax.random.key(seed)
        k1, k2, k3 = jax.random.split(key, 3)
        x = jax.random.normal(k1, (4, 256, D_MODEL), dtype=jnp.float32)
        norm_w = jnp.ones((D_MODEL,), dtype=jnp.float32)
        w_gv = jax.random.normal(k2, (2 * HIDDEN, D_MODEL), dtype=jnp.float32) * D_MODEL ** (-0.5)
        w_out = jax.random.normal(k3, (D_MODEL, HIDDEN), dtype=jnp.float32) * HIDDEN ** (-0.5)
        return {'x': x, 'norm_w': norm_w, 'w_gv': w_gv, 'w_out': w_out}
    _L3_ffn_all = _L3_ffn_setup()
    _L3_ffn_in = {k: v for k, v in _L3_ffn_all.items() if k in ('norm_w', 'w_gv', 'w_out')}
    del _L3_ffn_all
    return {'x': x, 'ctx_512': ctx_512, 'L0_xattn_Wq': _L0_xattn_in['Wq'], 'L0_xattn_Wkv_expand': _L0_xattn_in['Wkv_expand'], 'L0_xattn_Wout': _L0_xattn_in['Wout'], 'L0_attn_W_in': _L0_attn_in['W_in'], 'L0_attn_b_in': _L0_attn_in['b_in'], 'L0_attn_W_gate': _L0_attn_in['W_gate'], 'L0_attn_b_gate': _L0_attn_in['b_gate'], 'L0_attn_forget_lambda': _L0_attn_in['forget_lambda'], 'L0_ffn_SU_ug': _L0_ffn_in['SU_ug'], 'L0_ffn_SU_dp': _L0_ffn_in['SU_dp'], 'L0_ffn_Wscale_ug': _L0_ffn_in['Wscale_ug'], 'L0_ffn_Wscale_dp': _L0_ffn_in['Wscale_dp'], 'L0_ffn_W_up': _L0_ffn_in['W_up'], 'L0_ffn_W_gate': _L0_ffn_in['W_gate'], 'L0_ffn_W_down': _L0_ffn_in['W_down'], 'L1_xattn_Wq': _L1_xattn_in['Wq'], 'L1_xattn_w_kc_q': _L1_xattn_in['w_kc_q'], 'L1_xattn_w_kc_kv': _L1_xattn_in['w_kc_kv'], 'L1_xattn_W_qr': _L1_xattn_in['W_qr'], 'L1_xattn_W_kr': _L1_xattn_in['W_kr'], 'L1_xattn_Wo': _L1_xattn_in['Wo'], 'L1_attn_gamma': _L1_attn_in['gamma'], 'L1_attn_beta': _L1_attn_in['beta'], 'L1_attn_W1': _L1_attn_in['W1'], 'L1_attn_b1': _L1_attn_in['b1'], 'L1_attn_W2': _L1_attn_in['W2'], 'L1_attn_b2': _L1_attn_in['b2'], 'L1_attn_W3': _L1_attn_in['W3'], 'L1_attn_b3': _L1_attn_in['b3'], 'L1_attn_Wqkv': _L1_attn_in['Wqkv'], 'L1_attn_bqkv': _L1_attn_in['bqkv'], 'L1_attn_Wout': _L1_attn_in['Wout'], 'L1_attn_bout': _L1_attn_in['bout'], 'L1_ffn_router_w': _L1_ffn_in['router_w'], 'L1_ffn_gate_w': _L1_ffn_in['gate_w'], 'L1_ffn_up_w': _L1_ffn_in['up_w'], 'L1_ffn_down_w': _L1_ffn_in['down_w'], 'L2_xattn_Wq': _L2_xattn_in['Wq'], 'L2_xattn_Wkv_expand': _L2_xattn_in['Wkv_expand'], 'L2_xattn_Wout': _L2_xattn_in['Wout'], 'L2_attn_W_in': _L2_attn_in['W_in'], 'L2_attn_W_gate': _L2_attn_in['W_gate'], 'L2_attn_b_gate': _L2_attn_in['b_gate'], 'L2_attn_rms_w': _L2_attn_in['rms_w'], 'L2_attn_W_out': _L2_attn_in['W_out'], 'L2_ffn_gate_w': _L2_ffn_in['gate_w'], 'L2_ffn_w13': _L2_ffn_in['w13'], 'L2_ffn_w2': _L2_ffn_in['w2'], 'L2_ffn_sw13': _L2_ffn_in['sw13'], 'L2_ffn_sw2': _L2_ffn_in['sw2'], 'L3_xattn_Wq': _L3_xattn_in['Wq'], 'L3_xattn_w_kc_q': _L3_xattn_in['w_kc_q'], 'L3_xattn_w_kc_kv': _L3_xattn_in['w_kc_kv'], 'L3_xattn_W_qr': _L3_xattn_in['W_qr'], 'L3_xattn_W_kr': _L3_xattn_in['W_kr'], 'L3_xattn_Wo': _L3_xattn_in['Wo'], 'L3_attn_Wq': _L3_attn_in['Wq'], 'L3_attn_Wk': _L3_attn_in['Wk'], 'L3_attn_Wv': _L3_attn_in['Wv'], 'L3_attn_Wo': _L3_attn_in['Wo'], 'L3_attn_bo': _L3_attn_in['bo'], 'L3_ffn_norm_w': _L3_ffn_in['norm_w'], 'L3_ffn_w_gv': _L3_ffn_in['w_gv'], 'L3_ffn_w_out': _L3_ffn_in['w_out']}

def reference(x, ctx_512, L0_xattn_Wq, L0_xattn_Wkv_expand, L0_xattn_Wout, L0_attn_W_in, L0_attn_b_in, L0_attn_W_gate, L0_attn_b_gate, L0_attn_forget_lambda, L0_ffn_SU_ug, L0_ffn_SU_dp, L0_ffn_Wscale_ug, L0_ffn_Wscale_dp, L0_ffn_W_up, L0_ffn_W_gate, L0_ffn_W_down, L1_xattn_Wq, L1_xattn_w_kc_q, L1_xattn_w_kc_kv, L1_xattn_W_qr, L1_xattn_W_kr, L1_xattn_Wo, L1_attn_gamma, L1_attn_beta, L1_attn_W1, L1_attn_b1, L1_attn_W2, L1_attn_b2, L1_attn_W3, L1_attn_b3, L1_attn_Wqkv, L1_attn_bqkv, L1_attn_Wout, L1_attn_bout, L1_ffn_router_w, L1_ffn_gate_w, L1_ffn_up_w, L1_ffn_down_w, L2_xattn_Wq, L2_xattn_Wkv_expand, L2_xattn_Wout, L2_attn_W_in, L2_attn_W_gate, L2_attn_b_gate, L2_attn_rms_w, L2_attn_W_out, L2_ffn_gate_w, L2_ffn_w13, L2_ffn_w2, L2_ffn_sw13, L2_ffn_sw2, L3_xattn_Wq, L3_xattn_w_kc_q, L3_xattn_w_kc_kv, L3_xattn_W_qr, L3_xattn_W_kr, L3_xattn_Wo, L3_attn_Wq, L3_attn_Wk, L3_attn_Wv, L3_attn_Wo, L3_attn_bo, L3_ffn_norm_w, L3_ffn_w_gv, L3_ffn_w_out):
    import jax
    import jax.numpy as jnp

    def _L0_xattn_ref(q, latent_kv, Wq, Wkv_expand, Wout):
        import jax, jax.numpy as jnp
        import numpy as np
        B, S, H, NH, L = (2, 256, 256, 16, 64)
        HD = H // NH
        b, sq, _ = q.shape
        sk = latent_kv.shape[1]
        qp = q @ Wq.T
        kv = latent_kv @ Wkv_expand.T
        k, v = jnp.split(kv, 2, axis=-1)
        qh = qp.reshape(b, sq, NH, HD).transpose(0, 2, 1, 3)
        kh = k.reshape(b, sk, NH, HD).transpose(0, 2, 1, 3)
        vh = v.reshape(b, sk, NH, HD).transpose(0, 2, 1, 3)
        inv_sqrt_d = 1.0 / jnp.sqrt(jnp.float32(HD))
        scores = jnp.einsum('bhqd,bhkd->bhqk', qh, kh) * inv_sqrt_d
        causal = jnp.tril(jnp.ones((sq, sk), dtype=bool))
        scores = jnp.where(causal, scores, jnp.finfo(scores.dtype).min)
        attn = jax.nn.softmax(scores, axis=-1)
        out = jnp.einsum('bhqk,bhkd->bhqd', attn, vh)
        out = out.transpose(0, 2, 1, 3).reshape(b, sq, H)
        return out @ Wout.T

    def _L0_attn_ref(x, W_in, b_in, W_gate, b_gate, forget_lambda):
        import jax, jax.numpy as jnp
        import numpy as np
        C = 8.0

        def _linear_scan(alpha, xbeta):

            def combine(e1, e2):
                a1, b1 = e1
                a2, b2 = e2
                return (a2 * a1, a2 * b1 + b2)
            _, h = jax.lax.associative_scan(combine, (alpha, xbeta), axis=1)
            return h
        input_gate = jnp.einsum('btd,ed->bte', x, W_in) + b_in
        recurrence_gate = jnp.einsum('btd,ed->bte', x, W_gate) + b_gate
        alpha = jnp.exp(-C * jax.nn.softplus(forget_lambda) * jax.nn.sigmoid(recurrence_gate))
        beta = jnp.sqrt(1.0 - alpha ** 2 + 1e-06)
        xbeta = beta * jax.nn.sigmoid(input_gate) * x
        return _linear_scan(alpha, xbeta)

    def _L0_ffn_ref(input, SU_ug, SU_dp, Wscale_ug, Wscale_dp, W_up, W_gate, W_down):
        import jax, jax.numpy as jnp
        import numpy as np
        HIDDEN = 256
        INTER = 1024
        SCALE = 64.0

        def fwht(x):
            orig_shape = x.shape
            n = orig_shape[-1]
            x = x.reshape(-1, n)
            h = 1
            while h < n:
                x = x.reshape(-1, n // (2 * h), 2, h)
                a, b = (x[:, :, 0, :], x[:, :, 1, :])
                x = jnp.stack([a + b, a - b], axis=2).reshape(-1, n)
                h *= 2
            return (x / jnp.sqrt(jnp.asarray(n, x.dtype))).reshape(orig_shape)
        n = SU_ug.shape[0]
        x = input.reshape(-1, n)
        x = fwht(x * SU_ug) / SCALE
        x_up = x @ W_up.T * (Wscale_ug[:INTER] * SCALE)
        x_gate = x @ W_gate.T * (Wscale_ug[INTER:] * SCALE)
        x = jax.nn.silu(x_gate) * x_up
        x = fwht(x * SU_dp) / SCALE
        x = x @ W_down.T * (Wscale_dp * SCALE)
        return x.reshape(input.shape)

    def _L1_xattn_ref(hidden_q, kv_c, Wq, w_kc_q, w_kc_kv, W_qr, W_kr, Wo):
        import jax, jax.numpy as jnp
        import numpy as np
        B, S, L = (2, 128, 128)
        DIM_Q, H, K, D_C, D_CQ, R = (256, 16, 128, 64, 192, 64)

        def _rope_tables(length, dim):
            inv = 1.0 / 10000.0 ** (jnp.arange(0, dim, 2, dtype=jnp.float32) / dim)
            f = jnp.arange(length, dtype=jnp.float32)[:, None] * inv[None, :]
            sin = jnp.repeat(jnp.sin(f), 2, axis=-1)
            cos = jnp.repeat(jnp.cos(f), 2, axis=-1)
            return (sin, cos)

        def _rotate_half(x):
            half = x.shape[-1] // 2
            return jnp.concatenate([-x[..., half:], x[..., :half]], axis=-1)

        def _apply_rope(x, sin, cos):
            return x * cos + _rotate_half(x) * sin
        Bv, Sv, _ = hidden_q.shape
        _, Lv, _ = kv_c.shape
        q_hk = (hidden_q @ Wq.T).reshape(Bv, Sv, H, K)
        q_big = jnp.einsum('bshk,hkq->bshq', q_hk, w_kc_q)
        sin_q, cos_q = _rope_tables(Sv, D_CQ)
        q_big = _apply_rope(q_big, sin_q[None, :, None, :], cos_q[None, :, None, :])
        sin_k, cos_k = _rope_tables(Lv, D_C)
        kv_r = _apply_rope(kv_c, sin_k[None], cos_k[None])
        q_r = jnp.einsum('bshq,hqr->bhsr', q_big, W_qr)
        k_r = jnp.einsum('bld,hdr->bhlr', kv_r, W_kr)
        scores = jnp.einsum('bhsr,bhlr->bhsl', q_r, k_r)
        attn = jax.nn.softmax(scores, axis=-1)
        ctx_c = jnp.einsum('bhsl,bld->bhsd', attn, kv_r)
        ctx_lat = jnp.einsum('bhsd,hkd->bhsk', ctx_c, w_kc_kv)
        ctx = ctx_lat.transpose(0, 2, 1, 3).reshape(Bv, Sv, H * K)
        return ctx @ Wo.T

    def _L1_attn_ref(x, gamma, beta, W1, b1, W2, b2, W3, b3, Wqkv, bqkv, Wout, bout):
        import jax, jax.numpy as jnp
        import numpy as np
        import math
        D = 256
        K = 64
        NUM_HEADS = 32
        HEAD_DIM = K // NUM_HEADS
        SPARSITY = 0.1
        LN_EPS = 1e-05
        B, S, d = x.shape
        mu = jnp.mean(x, -1, keepdims=True)
        var = jnp.var(x, -1, keepdims=True)
        xn = (x - mu) * jax.lax.rsqrt(var + LN_EPS) * gamma + beta
        h = jnp.einsum('bsd,fd->bsf', xn, W1)
        pair = jax.nn.relu(h[:, :, None, :] - h[:, None, :, :] + b1)
        pair = jax.nn.relu(jnp.einsum('bijf,gf->bijg', pair, W2) + b2)
        sim = jnp.einsum('bijg,og->bijo', pair, W3)[..., 0] + b3[0]
        diag = jnp.arange(S)
        sim = sim.at[:, diag, diag].set(0.0)
        k_sparse = max(1, int(S * SPARSITY))
        _, top_idx = jax.lax.top_k(sim, k_sparse)
        mask = jnp.full((B, S, S), -jnp.inf, dtype=x.dtype)
        bidx = jnp.arange(B)[:, None, None]
        iidx = jnp.arange(S)[None, :, None]
        mask = mask.at[bidx, iidx, top_idx].set(0.0)
        qkv = jnp.einsum('bsd,ed->bse', xn, Wqkv) + bqkv
        q, k, v = jnp.split(qkv, 3, axis=-1)

        def heads(t):
            return t.reshape(B, S, NUM_HEADS, HEAD_DIM).transpose(0, 2, 1, 3)
        q, k, v = (heads(q), heads(k), heads(v))
        scores = jnp.einsum('bhid,bhjd->bhij', q, k) / math.sqrt(HEAD_DIM)
        scores = scores + mask[:, None, :, :]
        attn = jax.nn.softmax(scores, axis=-1)
        ao = jnp.einsum('bhij,bhjd->bhid', attn, v)
        ao = ao.transpose(0, 2, 1, 3).reshape(B, S, K)
        out = jnp.einsum('bsk,dk->bsd', ao, Wout) + bout
        return x + out

    def _L1_ffn_ref(hidden_states, router_w, gate_w, up_w, down_w):
        import jax, jax.numpy as jnp
        import numpy as np
        TOP_P = 0.9
        S, B, H, I, E = (256, 4, 256, 512, 8)

        def _top_p_weights(probs, top_p):
            order = jnp.argsort(-probs, axis=-1)
            sp = jnp.take_along_axis(probs, order, axis=-1)
            cum = jnp.cumsum(sp, axis=-1)
            exceed = cum > top_p
            first_idx = jnp.argmax(exceed, axis=-1)
            first = jnp.arange(probs.shape[-1])[None, :] == first_idx[:, None]
            keep = ~exceed | first
            kept = jnp.where(keep, sp, 0.0)
            t_idx = jnp.arange(probs.shape[0])[:, None]
            return jnp.zeros_like(probs).at[t_idx, order].set(kept)
        s, b, h = hidden_states.shape
        x = hidden_states.reshape(-1, h)
        probs = jax.nn.softmax(x @ router_w.T, axis=-1)
        w = _top_p_weights(probs, TOP_P)
        out = jnp.zeros_like(x)
        n_exp = router_w.shape[0]
        for e in range(n_exp):
            g = jax.nn.silu(x @ gate_w[e].T)
            u = x @ up_w[e].T
            y = g * u @ down_w[e].T
            out = out + y * w[:, e:e + 1]
        return out.reshape(s, b, h)

    def _L2_xattn_ref(q, latent_kv, Wq, Wkv_expand, Wout):
        import jax, jax.numpy as jnp
        import numpy as np
        B, S, H, NH, L = (2, 256, 256, 16, 64)
        HD = H // NH
        b, sq, _ = q.shape
        sk = latent_kv.shape[1]
        qp = q @ Wq.T
        kv = latent_kv @ Wkv_expand.T
        k, v = jnp.split(kv, 2, axis=-1)
        qh = qp.reshape(b, sq, NH, HD).transpose(0, 2, 1, 3)
        kh = k.reshape(b, sk, NH, HD).transpose(0, 2, 1, 3)
        vh = v.reshape(b, sk, NH, HD).transpose(0, 2, 1, 3)
        inv_sqrt_d = 1.0 / jnp.sqrt(jnp.float32(HD))
        scores = jnp.einsum('bhqd,bhkd->bhqk', qh, kh) * inv_sqrt_d
        causal = jnp.tril(jnp.ones((sq, sk), dtype=bool))
        scores = jnp.where(causal, scores, jnp.finfo(scores.dtype).min)
        attn = jax.nn.softmax(scores, axis=-1)
        out = jnp.einsum('bhqk,bhkd->bhqd', attn, vh)
        out = out.transpose(0, 2, 1, 3).reshape(b, sq, H)
        return out @ Wout.T

    def _L2_attn_ref(x, W_in, W_gate, b_gate, rms_w, W_out):
        import jax, jax.numpy as jnp
        import numpy as np
        DIM = 256
        HIDDEN = 256
        HEADS = 4
        HD = HIDDEN // HEADS
        EPS = 1e-06
        BATCH = 4
        SEQ = 256
        B, L, _ = x.shape
        xp = x @ W_in.T
        gates = xp @ W_gate.T + b_gate
        gates = gates.reshape(B, L, HEADS, 4 * HD).transpose(0, 2, 1, 3)
        i_g, f_g, o_g, c_t = jnp.split(gates, 4, axis=-1)
        i_g = jnp.exp(i_g)
        f_g = jax.nn.sigmoid(f_g)
        o_g = jax.nn.sigmoid(o_g)
        c_t = jnp.tanh(c_t)
        tm = lambda a: jnp.moveaxis(a, 2, 0)

        def step(c, g):
            i, f, o, cd = g
            c = f * c + i * cd
            c_norm = c * jax.lax.rsqrt(jnp.mean(c * c, axis=-1, keepdims=True) + EPS) * rms_w
            h = o * jnp.tanh(c_norm)
            return (c, h)
        c0 = jnp.zeros((B, HEADS, HD), dtype=x.dtype)
        _, hs = jax.lax.scan(step, c0, (tm(i_g), tm(f_g), tm(o_g), tm(c_t)))
        h_out = jnp.moveaxis(hs, 0, 1).reshape(B, L, HIDDEN)
        return h_out @ W_out.T

    def _L2_ffn_ref(hidden_states, gate_w, w13, w2, sw13, sw2):
        import jax, jax.numpy as jnp
        import numpy as np
        from jax import lax
        H = 256
        I = 176
        E = 16
        TOP_K = 6
        IS = 2 * I

        def _swiglu(x, w13_, w2_):
            gu = x @ w13_.T
            g, u = jnp.split(gu, 2, axis=-1)
            return jax.nn.silu(g) * u @ w2_.T
        B, S, Hd = hidden_states.shape
        x = hidden_states.reshape(-1, Hd)
        T = x.shape[0]
        scores = jax.nn.softmax(x @ gate_w.T, axis=-1)
        topk_w, topk_ids = lax.top_k(scores, TOP_K)
        topk_w = topk_w / (topk_w.sum(-1, keepdims=True) + 1e-20)
        combine = jnp.einsum('tk,tke->te', topk_w, jax.nn.one_hot(topk_ids, E, dtype=topk_w.dtype))

        def body(acc, ew):
            w13_e, w2_e, c_e = ew
            y = _swiglu(x, w13_e, w2_e)
            return (acc + c_e[:, None] * y, None)
        out, _ = lax.scan(body, jnp.zeros_like(x), (w13, w2, combine.T))
        out = out + _swiglu(x, sw13, sw2)
        return out.reshape(B, S, Hd)

    def _L3_xattn_ref(hidden_q, kv_c, Wq, w_kc_q, w_kc_kv, W_qr, W_kr, Wo):
        import jax, jax.numpy as jnp
        import numpy as np
        B, S, L = (2, 128, 128)
        DIM_Q, H, K, D_C, D_CQ, R = (256, 16, 128, 64, 192, 64)

        def _rope_tables(seq_len, dim, dtype):
            inv_freq = 1.0 / 10000.0 ** (jnp.arange(0, dim, 2, dtype=dtype) / dim)
            t = jnp.arange(seq_len, dtype=dtype)
            freqs = t[:, None] * inv_freq[None, :]
            sin = jnp.repeat(jnp.sin(freqs), 2, axis=-1)
            cos = jnp.repeat(jnp.cos(freqs), 2, axis=-1)
            return (sin, cos)

        def _rotate_half(x):
            h = x.shape[-1] // 2
            return jnp.concatenate([-x[..., h:], x[..., :h]], axis=-1)
        b, s, _ = hidden_q.shape
        l = kv_c.shape[1]
        q_hk = (hidden_q @ Wq.T).reshape(b, s, H, K)
        q_big = jnp.einsum('bshk,hkq->bshq', q_hk, w_kc_q)
        sin, cos = _rope_tables(l, D_C, kv_c.dtype)
        kv_rope = kv_c * cos[None] + _rotate_half(kv_c) * sin[None]
        q_r = jnp.einsum('bshq,hqr->bhsr', q_big, W_qr)
        k_r = jnp.einsum('bld,hdr->bhlr', kv_rope, W_kr)
        scores = jnp.einsum('bhsr,bhlr->bhsl', q_r, k_r)
        attn = jax.nn.softmax(scores, axis=-1)
        ctx_c = jnp.einsum('bhsl,bld->bhsd', attn, kv_rope)
        ctx_lat = jnp.einsum('bhsd,hkd->bshk', ctx_c, w_kc_kv)
        out = ctx_lat.reshape(b, s, H * K) @ Wo.T
        return out

    def _L3_attn_ref(x, Wq, Wk, Wv, Wo, bo):
        import jax, jax.numpy as jnp
        import numpy as np
        D_IN = 256
        D_OUT = 256
        NUM_HEADS = 16
        NUM_KV_GROUPS = 4
        GROUP_SIZE = NUM_HEADS // NUM_KV_GROUPS
        HEAD_DIM = D_OUT // NUM_HEADS
        b, n, _ = x.shape
        q = (x @ Wq).reshape(b, n, NUM_KV_GROUPS, GROUP_SIZE, HEAD_DIM)
        k = (x @ Wk).reshape(b, n, NUM_KV_GROUPS, HEAD_DIM)
        v = (x @ Wv).reshape(b, n, NUM_KV_GROUPS, HEAD_DIM)
        scale = 1.0 / np.sqrt(HEAD_DIM).astype(np.float32)
        scores = jnp.einsum('bqgsd,bkgd->bgsqk', q, k) * scale
        causal = jnp.arange(n)[:, None] < jnp.arange(n)[None, :]
        scores = jnp.where(causal, -jnp.inf, scores)
        attn = jax.nn.softmax(scores, axis=-1)
        ctx = jnp.einsum('bgsqk,bkgd->bqgsd', attn, v)
        ctx = ctx.reshape(b, n, D_OUT)
        return ctx @ Wo + bo

    def _L3_ffn_ref(x, norm_w, w_gv, w_out):
        import jax, jax.numpy as jnp
        import numpy as np
        D_MODEL = 256
        HIDDEN = 4 * D_MODEL
        EPS = 1e-05
        QB = 127.0

        def _ste(orig, quant):
            return orig + jax.lax.stop_gradient(quant - orig)

        def _act_quant(a):
            scale = QB / jnp.clip(jnp.max(jnp.abs(a), axis=-1, keepdims=True), 1e-05)
            q = jnp.clip(jnp.round(a * scale), -QB, QB) / scale
            return _ste(a, q)

        def _weight_quant(w):
            s = jnp.clip(jnp.mean(jnp.abs(w)), 1e-05)
            q = jnp.clip(jnp.round(w / s), -1.0, 1.0) * s
            return _ste(w, q)

        def _bitlinear(x, w):
            return jnp.einsum('bsd,od->bso', _act_quant(x), _weight_quant(w))

        def _rmsnorm(x, g):
            var = jnp.mean(jnp.square(x), axis=-1, keepdims=True)
            return x * jax.lax.rsqrt(var + EPS) * g
        residual = x
        h = _rmsnorm(x, norm_w)
        gv = _bitlinear(h, w_gv)
        value, gate = jnp.split(gv, 2, axis=-1)
        h = value * jax.nn.silu(gate)
        h = _bitlinear(h, w_out)
        return residual + h
    x = x + _L0_xattn_ref(_layernorm(x, axis=-1), ctx_512, L0_xattn_Wq, L0_xattn_Wkv_expand, L0_xattn_Wout)
    x = x + _L0_attn_ref(_layernorm(x, axis=-1), L0_attn_W_in, L0_attn_b_in, L0_attn_W_gate, L0_attn_b_gate, L0_attn_forget_lambda)
    x = x + _L0_ffn_ref(_layernorm(x, axis=-1), L0_ffn_SU_ug, L0_ffn_SU_dp, L0_ffn_Wscale_ug, L0_ffn_Wscale_dp, L0_ffn_W_up, L0_ffn_W_gate, L0_ffn_W_down)
    x = x + _L1_xattn_ref(_layernorm(x, axis=-1), ctx_512, L1_xattn_Wq, L1_xattn_w_kc_q, L1_xattn_w_kc_kv, L1_xattn_W_qr, L1_xattn_W_kr, L1_xattn_Wo)
    x = x + _L1_attn_ref(_layernorm(x, axis=-1), L1_attn_gamma, L1_attn_beta, L1_attn_W1, L1_attn_b1, L1_attn_W2, L1_attn_b2, L1_attn_W3, L1_attn_b3, L1_attn_Wqkv, L1_attn_bqkv, L1_attn_Wout, L1_attn_bout)
    x = x + _L1_ffn_ref(_layernorm(x, axis=-1), L1_ffn_router_w, L1_ffn_gate_w, L1_ffn_up_w, L1_ffn_down_w)
    x = x + _L2_xattn_ref(_layernorm(x, axis=-1), ctx_512, L2_xattn_Wq, L2_xattn_Wkv_expand, L2_xattn_Wout)
    x = x + _L2_attn_ref(_layernorm(x, axis=-1), L2_attn_W_in, L2_attn_W_gate, L2_attn_b_gate, L2_attn_rms_w, L2_attn_W_out)
    x = x + _L2_ffn_ref(_layernorm(x, axis=-1), L2_ffn_gate_w, L2_ffn_w13, L2_ffn_w2, L2_ffn_sw13, L2_ffn_sw2)
    x = x + _L3_xattn_ref(_layernorm(x, axis=-1), ctx_512, L3_xattn_Wq, L3_xattn_w_kc_q, L3_xattn_w_kc_kv, L3_xattn_W_qr, L3_xattn_W_kr, L3_xattn_Wo)
    x = x + _L3_attn_ref(_layernorm(x, axis=-1), L3_attn_Wq, L3_attn_Wk, L3_attn_Wv, L3_attn_Wo, L3_attn_bo)
    x = x + _L3_ffn_ref(_layernorm(x, axis=-1), L3_ffn_norm_w, L3_ffn_w_gv, L3_ffn_w_out)
    return x

_drawn_inputs = setup_inputs


def setup_inputs(seed=0):
    import zlib

    import numpy as np

    out = dict(_drawn_inputs(seed))
    spreads = {'L0_attn_b_in': (0.0, 0.8),
     'L0_attn_b_gate': (0.0, 0.8),
     'L1_attn_gamma': (1.0, 0.6),
     'L1_attn_beta': (0.0, 0.8),
     'L1_attn_b1': (0.0, 0.8),
     'L1_attn_b2': (0.0, 0.667),
     'L1_attn_bqkv': (0.0, 0.8),
     'L1_attn_bout': (0.0, 0.362),
     'L2_attn_b_gate': (0.0, 0.8),
     'L2_attn_rms_w': (1.0, 0.6),
     'L3_ffn_norm_w': (1.0, 0.6)}
    factors = {'L0_xattn_Wq': 8.0,
     'L0_ffn_Wscale_ug': 5.216,
     'L0_ffn_Wscale_dp': 7.133,
     'L1_attn_W1': 5.963,
     'L1_attn_W2': 5.916,
     'L1_attn_W3': 5.876,
     'L1_attn_Wqkv': 4.003,
     'L1_attn_Wout': 3.68,
     'L1_ffn_router_w': 8.0,
     'L1_ffn_gate_w': 8.0,
     'L1_ffn_up_w': 8.0,
     'L1_ffn_down_w': 8.0,
     'L2_xattn_Wq': 8.0,
     'L2_xattn_Wkv_expand': 4.571,
     'L2_xattn_Wout': 4.616,
     'L2_ffn_gate_w': 8.0,
     'L2_ffn_w13': 8.0,
     'L2_ffn_w2': 8.0,
     'L2_ffn_sw13': 7.262,
     'L2_ffn_sw2': 7.243,
     'L3_attn_bo': 64.0,
     'L2_attn_W_in': 8.0,
     'L2_attn_W_gate': 8.0,
     'L2_attn_W_out': 6.139,
     'L3_attn_Wq': 4.027,
     'L3_attn_Wk': 3.993,
     'L3_ffn_w_gv': 3.154,
     'L3_ffn_w_out': 3.133}
    for name, (base, spread) in spreads.items():
        noise = np.random.default_rng([zlib.crc32(name.encode()), seed]).standard_normal(out[name].shape)
        drawn = base * np.exp(spread * noise) if base else spread * noise
        out[name] = jnp.asarray(drawn.astype(out[name].dtype))
    for name, factor in factors.items():
        out[name] = (out[name] * factor).astype(out[name].dtype)
    return out
```

```python
from contextlib import ExitStack

import numpy as np

import concourse.bass as bass
from concourse import mybir

F32 = mybir.dt.float32
BF16 = mybir.dt.bfloat16
ALU = mybir.AluOpType
ACT = mybir.ActivationFunctionType
AXX = mybir.AxisListType.X
ds = bass.ds

B, S, D = 32, 32, 256
P = 128
TOK = B * S
NT = TOK // P
BT = P // S
LC, DC = 257, 64
NEG = -1.0e30


class Stage:

    def __init__(self, nc, name):
        self.nc, self.name, self.sems, self.ctx = nc, name, {}, ExitStack()

    def __enter__(self):
        return self

    def sb(self, name, shape, dt=F32):
        return self.ctx.enter_context(self.nc.sbuf_tensor(f"{self.name}_{name}", shape, dt))

    def ps(self, name, shape, dt=F32):
        return self.ctx.enter_context(self.nc.psum_tensor(f"{self.name}_{name}", shape, dt))

    def sem(self, names):
        out = []
        for n in names.split():
            self.sems[n] = self.nc.alloc_semaphore(f"{self.name}_{n}")
            out.append(self.sems[n])
        return out if len(out) > 1 else out[0]

    def pair(self, name):
        return [self.sem(f"{name}0"), self.sem(f"{name}1")]

    def __exit__(self, *why):
        if why[0] is None:
            self.nc.clear_and_free_semaphores(list(self.sems.values()))
            self.nc.all_engine_barrier()
            self.ctx.close()
        return False


class LayerNorm:

    def __init__(self, g, st, psT, keep=None, eps=1e-5, src=None, affine=None, pre=""):
        self.g, self.psT, self.keep, self.eps, self.affine = g, psT, keep, eps, affine
        self.src = g.X if src is None else src
        self.st = st.sb(pre + "lnst", [P, NT, 6])
        self.mv = st.sb(pre + "lnmv", [P, NT, 2])
        self.ve = st.sb(pre + "lnve", [P, NT])
        self.rs = st.sb(pre + "lnrs", [P, NT])
        self.xn = st.sb(pre + "lnxn", [P, 2, D]) if keep is None else None
        (self.stat, self.aggr, self.vared, self.rstd) = st.sem(f"{pre}ln_stat {pre}ln_aggr {pre}ln_vared {pre}ln_rstd")
        self.normed = st.pair(pre + "ln_normed")
        self.turned = st.pair(pre + "ln_turned")
        self.ready = st.pair(pre + "ln_ready")

    def vector(self, v):
        X, st, mv = self.src, self.st, self.mv
        with v.Fori(0, NT) as t:
            v.bn_stats(st[:, ds(t, 1), :], X[:, ds(t, 1), :]).then_inc(self.stat, 1)
        v.wait_ge(self.stat, NT)
        for t in range(NT):
            v.bn_aggr(mv[:, t, :], st[:, t, :]).then_inc(self.aggr, 1)
        v.wait_ge(self.aggr, NT)
        v.tensor_scalar(self.ve[:, :], mv[:, :, 1], self.eps, None, ALU.add).then_inc(self.vared, 1)
        v.wait_ge(self.rstd, 1)
        with v.Fori(0, NT // 2) as i:
            for u in range(2):
                t = 2 * i + u
                if self.keep is None:
                    v.wait_ge(self.turned[u], i + 1)
                    dst = self.xn[:, u:u + 1, :]
                else:
                    dst = self.keep[:, ds(t, 1), :]
                v.tensor_scalar(dst, X[:, ds(t, 1), :], mv[:, ds(t, 1), 0:1].rearrange("p a b -> p (a b)"),
                                self.rs[:, ds(t, 1)], ALU.subtract, ALU.mult).then_inc(self.normed[u], 1)

    def gpsimd(self, p):
        p.wait_ge(self.vared, 1)
        p.tensor_tensor(self.rs[:, :], self.ve[:, :], self.g.mhalf[:, 0:NT], ALU.pow).then_inc(self.rstd, 1)

    def tensor(self, pe):
        if self.keep is None:
            for u in range(2):
                pe.sem_inc(self.turned[u], 1)
        with pe.Fori(0, NT // 2) as i:
            for u in range(2):
                pe.wait_ge(self.normed[u], i + 1)
                pe.wait_ge(self.ready[u], i + 1)
                for c in range(2):
                    src = self.xn[:, u, c * P:(c + 1) * P]
                    mm = pe.transpose(self.psT[u][:, c * P:(c + 1) * P], src, self.g.ident[:, :])
                mm.then_inc(self.turned[u], 1)

    def scalar(self, a):
        for u in range(2):
            a.sem_inc(self.ready[u], 1)
        with a.Fori(0, NT // 2) as i:
            for u in range(2):
                a.wait_ge(self.turned[u], i + 2)
                if self.affine is not None:
                    for c in range(2):
                        ins = a.activation(self.g.xnT[:, c, ds((2 * i + u) * P, P)], self.psT[u][:, c * P:(c + 1) * P],
                                           ACT.Identity, scale=self.affine[:, c:c + 1], bias=self.affine[:, 2 + c:3 + c])
                    ins.then_inc(self.ready[u], 1)
                    continue
                a.activation(self.g.xnT[:, :, ds((2 * i + u) * P, P)],
                             self.psT[u][:, 0:2 * P].rearrange("p (c n) -> p c n", c=2), ACT.Copy).then_inc(self.ready[u], 1)

    def wait(self, eng):
        for u in range(2):
            eng.wait_ge(self.ready[u], NT // 2 + 1)


class Attention:

    def __init__(self, g, st, name, heads, hd, w, kv, kv_rows, kv_chunks, hmask, mask, bias={}):
        self.g, self.NH, self.HD, self.w, self.kv, self.KR, self.KC = g, heads, hd, w, kv, kv_rows, kv_chunks
        self.hmask, self.mask, self.bias = hmask, mask, bias
        self.A = heads * hd
        self.FC = max(1, self.A // P)
        self.R = self.A // self.FC
        self.HPC = heads // self.FC
        self.SW = heads * S
        self.TC = self.SW // P
        self.scale = 1.0 / float(np.sqrt(np.float32(hd)))
        A, FC, R, SW, TC = self.A, self.FC, self.R, self.SW, self.TC
        self.qT = st.sb("qT", [R, 2, FC, P])
        self.Kbd = st.sb("Kbd", [R, FC, BT, self.HPC * S])
        self.kvr = st.sb("kvr", [kv_rows, 2, kv_chunks, BT * 4 * S])
        self.sc = st.sb("sc", [P, 2, SW])
        self.mx = st.sb("mx", [P, heads])
        self.sm = st.sb("sm", [P, 2, heads])
        self.rinv = st.sb("rinv", [P, heads])
        self.PT = st.sb("PT", [P, TC, P])
        self.Vbd = st.sb("Vbd", [P, 2, BT, A])
        self.ao = st.sb("ao", [P, A])
        self.aoT = st.sb("aoT", [R, FC, P])
        self.psQ = st.ps("psQ", [P, 512])
        self.psK = st.ps("psK", [P, 512])
        self.psS = st.ps("psS", [P, SW])
        self.psT = st.ps("psT", [P, SW])
        self.psV = st.ps("psV", [P, max(BT * A, 512)])
        self.psO = st.ps("psO", [P, 512])
        self.s = {n: st.sem("at_" + n) for n in
                  "kvr kvr_free qk q_ready kbd scored masked maxed shifted exped summed turned pt "
                  "vrep vbd pv rin normed aot aot_ready projected added stood".split()}

    def gpsimd(self, p):
        s = self.s
        with p.Fori(0, NT // 2) as i:
            for u in range(2):
                t = 2 * i + u
                p.wait_ge(s["kvr_free"], t + 1)
                for c in range(self.KC):
                    src = self.kv[0:self.KR, c, ds(t * P, P)] if self.KC > 1 else self.kv[0:self.KR, ds(t * P, P)]
                    dst = self.kvr[:, u, c, :].rearrange("p (b r s) -> p b r s", b=BT, r=4)
                    x = src.rearrange("p (b s) -> p b s", b=BT).unsqueeze(2).to_broadcast([self.KR, BT, 4, S])
                    ins = p.tensor_copy(dst, x)
                    ins.then_inc(s["kvr"], 1)

    @staticmethod
    def over_tiles(eng, step):
        with eng.Fori(0, NT // 2 - 1) as i:
            step(0, 2 * i)
            step(1, 2 * i + 1)
        step(0, NT - 2)

    def tensor(self, pe):
        g, s, w = self.g, self.s, self.w
        R, FC, KC, A, TC = self.R, self.FC, self.KC, self.A, self.TC
        bias = self.bias

        def group(out, pairs):
            for n, (l, r) in enumerate(pairs):
                mm = pe.matmul(out, l, r, start=(n == 0), stop=(n == len(pairs) - 1))
            return mm

        for _ in range(2):
            pe.sem_inc(s["kvr_free"], 1)
        def inputs(u, t):
            if not isinstance(t, int) or t >= 1:
                pe.wait_ge(s["aot_ready"], t)
            for m in range(FC):
                pairs = [(w["q"][:, c, m * R:(m + 1) * R], g.xnT[:, c, ds(t * P, P)]) for c in range(2)]
                if "q" in bias:
                    pairs.append((bias["q"][0:1, m * R:(m + 1) * R], g.ones[0:1, 0:P]))
                group(self.psQ[0:R, m * P:(m + 1) * P], pairs)
            for m in range(FC):
                pairs = []
                for c in range(KC):
                    src = self.kv[0:self.KR, c, ds(t * P, P)] if KC > 1 else self.kv[0:self.KR, ds(t * P, P)]
                    pairs.append((w["k"][0:self.KR, c, m * R:(m + 1) * R], src))
                if "k" in bias:
                    pairs.append((bias["k"][0:1, m * R:(m + 1) * R], g.ones[0:1, 0:P]))
                mm = group(self.psK[0:R, m * P:(m + 1) * P], pairs)
            mm.then_inc(s["qk"], 1)
            pe.wait_ge(s["kvr"], KC * (t + 1))
            pe.wait_ge(s["vbd"], t + 1)
            for b in range(BT):
                pairs = [(self.kvr[:, u, c, b * P:(b + 1) * P], w["v"][0:self.KR, c, :]) for c in range(KC)]
                if "v" in bias:
                    pairs.append((g.ones[0:1, 0:P], bias["v"][0:1, :]))
                mm = group(self.psV[:, b * A:(b + 1) * A], pairs)
            mm.then_inc(s["vrep"], 1)

        def scores(u, t):
            pe.wait_ge(s["vbd"], t + 2)
            pe.sem_inc(s["kvr_free"], 1)
            pe.wait_ge(s["q_ready"], t + 1)
            pe.wait_ge(s["kbd"], t + 1)
            pe.wait_ge(s["masked"], t + 1)
            W = self.HPC * S
            if A < P:
                pe.sem_inc(s["stood"], 1)
            for b in range(BT):
                for m in range(FC):
                    for n in range(0, W, 512):
                        k = min(512, W - n)
                        mm = pe.matmul(self.psS[b * S:(b + 1) * S, m * W + n:m * W + n + k],
                                       self.qT[:, u, m, b * S:(b + 1) * S], self.Kbd[:, m, b, n:n + k],
                                       start=True, stop=True)
            mm.then_inc(s["scored"], 1)

        def turn(u, t):
            pe.wait_ge(s["exped"], t + 1)
            pe.wait_ge(s["pt"], t + 1)
            for c in range(TC):
                mm = pe.transpose(self.psT[:, c * P:(c + 1) * P], self.sc[:, u, c * P:(c + 1) * P], g.ident[:, :])
            mm.then_inc(s["turned"], 1)

        def weigh(u, t):
            pe.wait_ge(s["pt"], t + 2)
            pe.wait_ge(s["vbd"], t + 2)
            pe.wait_ge(s["added"], t + 1)
            V = 4 * self.HD
            for b in range(BT):
                for c in range(TC):
                    mm = pe.matmul(self.psO[b * S:(b + 1) * S, c * V:(c + 1) * V],
                                   self.PT[:, c, b * S:(b + 1) * S], self.Vbd[:, u, b, c * V:(c + 1) * V],
                                   start=True, stop=True)
            mm.then_inc(s["pv"], 1)

        def back(u, t):
            pe.wait_ge(s["normed"], t + 1)
            if A < P:
                pe.sem_inc(s["stood"], 1)
            for m in range(FC):
                mm = pe.transpose(self.psQ[0:R, m * P:(m + 1) * P], self.ao[:, m * R:(m + 1) * R], g.ident[:, :])
            mm.then_inc(s["aot"], 1)
            pe.wait_ge(s["aot_ready"], t + 2)
            pairs = [(self.aoT[:, m, :], w["o"][0:R, m, :]) for m in range(FC)]
            if "o" in bias:
                pairs.append((g.ones[0:1, 0:P], bias["o"][0:1, :]))
            group(self.psO[:, 256:512], pairs).then_inc(s["projected"], 1)

        def step(u, t):
            turn(u, t)
            inputs(1 - u, t + 1)
            weigh(u, t)
            scores(1 - u, t + 1)
            back(u, t)

        inputs(0, 0)
        scores(0, 0)
        self.over_tiles(pe, step)
        turn(1, NT - 1)
        weigh(1, NT - 1)
        back(1, NT - 1)

    def scalar(self, a):
        s, R, FC = self.s, self.R, self.FC
        a.sem_inc(s["aot_ready"], 1)
        a.sem_inc(s["pt"], 1)

        def keep_q(u, t):
            a.wait_ge(s["qk"], t + 1)
            a.activation(self.qT[:, u, :, :].rearrange("p f n -> p (f n)"), self.psQ[0:R, 0:FC * P], ACT.Copy,
                         scale=self.scale).then_inc(s["q_ready"], 1)

        def exponentials(u, t):
            a.wait_ge(s["shifted"], t + 1)
            a.activation(self.sc[:, u, :], self.sc[:, u, :], ACT.Exp).then_inc(s["exped"], 1)

        def keep_turned(t):
            a.wait_ge(s["turned"], t + 1)
            a.activation(self.PT[:, :, :].rearrange("p c n -> p (c n)"), self.psT[:, :], ACT.Copy).then_inc(s["pt"], 1)

        def keep_output(t):
            a.wait_ge(s["aot"], t + 1)
            a.activation(self.aoT[:, :, :].rearrange("p c n -> p (c n)"), self.psQ[0:R, 0:FC * P],
                         ACT.Copy).then_inc(s["aot_ready"], 1)

        def step(u, t):
            keep_turned(t)
            keep_q(1 - u, t + 1)
            keep_output(t)
            exponentials(1 - u, t + 1)

        keep_q(0, 0)
        exponentials(0, 0)
        self.over_tiles(a, step)
        keep_turned(NT - 1)
        keep_output(NT - 1)

    def vector(self, v):
        g, s, R, FC, NH = self.g, self.s, self.R, self.FC, self.NH
        for n in ("vbd", "masked", "added"):
            v.sem_inc(s[n], 1)

        def spread(u, t):
            v.wait_ge(s["qk"], t + 1)
            for m in range(FC):
                k = self.psK[0:R, m * P:(m + 1) * P].rearrange("p (b s) -> p b s", b=BT)
                ins = v.tensor_tensor(
                    self.Kbd[:, m, :, :].rearrange("p b (h s) -> p b h s", s=S),
                    k.unsqueeze(2).to_broadcast([R, BT, self.HPC, S]),
                    self.hmask[0:R, 0:self.HPC].unsqueeze(1).unsqueeze(3).to_broadcast([R, BT, self.HPC, S]),
                    ALU.mult)
            ins.then_inc(s["kbd"], 1)
            v.wait_ge(s["vrep"], t + 1)
            G = BT * self.TC
            v.tensor_tensor(self.Vbd[:, u, :, :].rearrange("p b (c r e) -> p (b c) r e", r=4, e=self.HD),
                            self.psV[:, 0:BT * self.A].rearrange("p (g r e) -> p g r e", r=4, e=self.HD),
                            g.vmask.unsqueeze(1).unsqueeze(3).to_broadcast([P, G, 4, self.HD]),
                            ALU.mult).then_inc(s["vbd"], 1)

        def shift(u, t):
            sc3 = self.sc[:, u, :].rearrange("p (h s) -> p h s", s=S)
            v.wait_ge(s["scored"], t + 1)
            mk = self.mask(t)
            v.tensor_tensor(sc3, self.psS[:, :].rearrange("p (h s) -> p h s", s=S),
                            mk.to_broadcast([P, NH, S]), ALU.add).then_inc(s["masked"], 1)
            v.wait_ge(s["masked"], t + 2)
            v.tensor_reduce(self.mx[:, :], sc3, AXX, ALU.max).then_inc(s["maxed"], 1)
            v.wait_ge(s["maxed"], t + 1)
            v.tensor_tensor(sc3, sc3, self.mx[:, :].unsqueeze(2).to_broadcast([P, NH, S]),
                            ALU.subtract).then_inc(s["shifted"], 1)

        def normalise(u, t):
            sc3 = self.sc[:, u, :].rearrange("p (h s) -> p h s", s=S)
            v.wait_ge(s["exped"], t + 1)
            v.tensor_reduce(self.sm[:, u, :], sc3, AXX, ALU.add).then_inc(s["summed"], 1)
            v.wait_ge(s["summed"], t + 1)
            v.reciprocal(self.rinv[:, :], self.sm[:, u, :]).then_inc(s["rin"], 1)
            v.wait_ge(s["rin"], t + 1)
            v.wait_ge(s["pv"], t + 1)
            v.tensor_tensor(self.ao[:, :].rearrange("p (h e) -> p h e", h=NH),
                            self.psO[:, 0:self.A].rearrange("p (h e) -> p h e", h=NH),
                            self.rinv[:, :].unsqueeze(2).to_broadcast([P, NH, self.HD]),
                            ALU.mult).then_inc(s["normed"], 1)

        def add(u, t):
            v.wait_ge(s["projected"], t + 1)
            x = g.X[:, ds(t, 1), :]
            v.tensor_tensor(x, x, self.psO[:, 256:512].unsqueeze(1), ALU.add).then_inc(s["added"], 1)

        def step(u, t):
            spread(1 - u, t + 1)
            normalise(u, t)
            shift(1 - u, t + 1)
            add(u, t)

        spread(0, 0)
        shift(0, 0)
        self.over_tiles(v, step)
        normalise(1, NT - 1)
        add(1, NT - 1)


def gated_recurrence_stage(nc, g):
    wi, wg, vec = g.w["a0in"], g.w["a0gate"], g.w["a0vec"]
    with Stage(nc, "a0") as st:
        SR, SI, AL, BE = [st.sb(n, [P, 2, TOK]) for n in ("rec", "inp", "alpha", "beta")]
        HT = st.sb("hT", [P, 2, TOK])
        ps = [st.ps(f"gate{n}", [P, 512]) for n in range(4)]
        pst = [st.ps(f"turn{n}", [P, 512]) for n in range(2)]
        ln = LayerNorm(g, st, pst)
        sp = st.sb("sp", [P, 8, 2])
        gated, opened, spd, spa, alphad, squared, rooted, fed, scanned, turned, added = st.sem(
            "gated opened softplus abs_exp alpha squared rooted fed scanned turned added")
        groups = [(gate, m, n) for gate in (1, 0) for m in range(2) for n in range(2)]
        with nc.Block() as block:
            @block.tensor
            def _(pe):
                ln.tensor(pe)
                ln.wait(pe)
                for k, (gate, m, n) in enumerate(groups):
                    if k >= 4:
                        pe.wait_ge(opened, k - 3)
                    w = wg if gate else wi
                    for c in range(2):
                        mm = pe.matmul(ps[k % 4][:, :], w[:, c, m * P:(m + 1) * P], g.xnT[:, c, n * 512:(n + 1) * 512],
                                       start=(c == 0), stop=(c == 1))
                    mm.then_inc(gated, 1)
                for t in range(NT):
                    pe.wait_ge(scanned, 2)
                    if t >= 2:
                        pe.wait_ge(added, t - 1)
                    for c in range(2):
                        mm = pe.transpose(pst[t % 2][:, c * P:(c + 1) * P], HT[:, c, t * P:(t + 1) * P], g.ident[:, :])
                    mm.then_inc(turned, 1)

            @block.scalar
            def _(a):
                ln.scalar(a)
                a.wait_ge(spa, 1)
                a.activation(sp[:, 1, :], sp[:, 0, :], ACT.Exp, scale=-1.0).then_inc(spa, 1)
                for k, (gate, m, n) in enumerate(groups):
                    a.wait_ge(gated, k + 1)
                    dst = (SR if gate else SI)[:, m, n * 512:(n + 1) * 512]
                    col = 2 * gate + m
                    a.activation(dst, ps[k % 4][:, :], ACT.Sigmoid, bias=vec[:, col:col + 1]).then_inc(opened, 1)
                a.wait_ge(opened, 4)
                a.wait_ge(spd, SP_STEPS)
                for m in range(2):
                    a.activation(AL[:, m, :], SR[:, m, :], ACT.Exp, scale=sp[:, 7, m:m + 1]).then_inc(alphad, 1)
                for m in range(2):
                    a.wait_ge(squared, 2 * m + 2)
                    a.activation(BE[:, m, :], BE[:, m, :], ACT.Sqrt).then_inc(rooted, 1)

            @block.gpsimd
            def _(p):
                ln.gpsimd(p)
                ln.wait(p)
                for m in range(2):
                    p.wait_ge(opened, 6 + 2 * m)
                    p.tensor_tensor(SI[:, m, :], SI[:, m, :], g.xnT[:, m, :], ALU.mult).then_inc(fed, 1)

            @block.vector
            def _(v):
                ln.vector(v)
                lam = vec[:, 4:6]
                v.tensor_scalar(sp[:, 0, :], lam, -1.0, None, ALU.mult).then_inc(spd, 1)
                v.wait_ge(spd, 1)
                v.tensor_tensor(sp[:, 0, :], sp[:, 0, :], lam, ALU.max).then_inc(spa, 1)
                v.wait_ge(spa, 2)
                steps = [1]

                def link(ins):
                    ins.then_inc(spd, 1)
                    steps[0] += 1
                    v.wait_ge(spd, steps[0])

                link(v.tensor_scalar(sp[:, 2, :], sp[:, 1, :], 2.0, None, ALU.add))
                link(v.reciprocal(sp[:, 3, :], sp[:, 2, :]))
                link(v.tensor_tensor(sp[:, 4, :], sp[:, 1, :], sp[:, 3, :], ALU.mult))
                link(v.tensor_tensor(sp[:, 5, :], sp[:, 4, :], sp[:, 4, :], ALU.mult))
                link(v.tensor_scalar(sp[:, 6, :], sp[:, 5, :], 1.0 / 19, 1.0 / 17, ALU.mult, ALU.add))
                for k in (15, 13, 11, 9, 7, 5, 3, 1):
                    link(v.tensor_tensor(sp[:, 6, :], sp[:, 6, :], sp[:, 5, :], ALU.mult))
                    link(v.tensor_scalar(sp[:, 6, :], sp[:, 6, :], 1.0 / k, None, ALU.add))
                link(v.tensor_tensor(sp[:, 6, :], sp[:, 6, :], sp[:, 4, :], ALU.mult))
                link(v.tensor_scalar(sp[:, 2, :], lam, 0.0, -8.0, ALU.max, ALU.mult))
                link(v.scalar_tensor_tensor(out=sp[:, 7, :], in0=sp[:, 6, :], scalar=-16.0, in1=sp[:, 2, :],
                                            op0=ALU.mult, op1=ALU.add))
                assert steps[0] == SP_STEPS
                for m in range(2):
                    v.wait_ge(alphad, m + 1)
                    v.scalar_tensor_tensor(out=BE[:, m, :], in0=AL[:, m, :], scalar=-1.0, in1=AL[:, m, :],
                                           op0=ALU.mult, op1=ALU.mult).then_inc(squared, 1)
                    v.wait_ge(squared, 2 * m + 1)
                    v.tensor_scalar(BE[:, m, :], BE[:, m, :], 1.0, 1e-6, ALU.add, ALU.add).then_inc(squared, 1)
                for m in range(2):
                    v.memset(AL[:, m, :].rearrange("p (b s) -> p b s", s=S)[:, :, 0:1], 0.0).then_inc(squared, 1)
                    v.wait_ge(rooted, m + 1)
                    v.wait_ge(fed, m + 1)
                    v.tensor_tensor(BE[:, m, :], BE[:, m, :], SI[:, m, :], ALU.mult).then_inc(squared, 1)
                    v.wait_ge(squared, 6 + 2 * m)
                    v.tensor_tensor_scan(HT[:, m, :], AL[:, m, :], BE[:, m, :], 0.0, ALU.mult,
                                         ALU.add).then_inc(scanned, 1)
                for t in range(NT):
                    v.wait_ge(turned, t + 1)
                    v.tensor_tensor(g.X[:, t, :], g.X[:, t, :], pst[t % 2][:, 0:D], ALU.add).then_inc(added, 1)


SP_STEPS = 1 + 5 + 16 + 3


class GatedFFN:

    def __init__(self, g, st, J, stream, src, resident_down=None, scales=None, spread=None):
        self.g, self.J, self.stream, self.src = g, J, stream, src
        self.down, self.scales, self.spread = resident_down, scales, spread
        self.WW = 512 if resident_down is not None else 768
        self.W = st.sb("W", [P, 2, self.WW])
        self.sg = st.sb("sg", [P, 2, 512])
        self.h = st.sb("h", [P, 2, 512])
        self.acc = [st.ps(f"acc{n}", [P, 512]) for n in range(4)]
        self.psG, self.psU = st.ps("psG", [P, 512]), st.ps("psU", [P, 512])
        self.psB = st.ps("psB", [P, 512]) if spread else None
        self.loaded = st.pair("ff_loaded")
        self.s = {n: st.sem("ff_" + n) for n in "gate silu up mult tmp half tile".split()}
        self.final = st.sem("ff_added")

    def tiles(self, eng, body):
        if self.scales:
            for j in range(self.J):
                body(j, j % 2, j // 2 + 1)
            return
        body(0, 0, 1)
        pairs = (self.J - 1) // 2
        with eng.Fori(0, pairs) as i:
            body(1 + 2 * i, 1, i + 1)
            body(2 + 2 * i, 0, i + 2)
        if self.J % 2 == 0:
            body(self.J - 1, 1, pairs + 1)

    def sync(self, sp):
        def body(j, slot, n):
            sp.wait_ge(self.s["half"], 2 * j + 2)
            src = self.stream[j, :, :] if isinstance(j, int) else \
                self.stream[ds(j, 1), :, :].rearrange("o p n -> (o p) n")
            sp.dma_start(self.W[:, slot, :], src).then_inc(self.loaded[slot], 16)
        self.tiles(sp, body)

    def tensor(self, pe):
        s = self.s
        pe.sem_inc(s["half"], 4)

        def body(j, slot, loads):
            pe.wait_ge(self.loaded[slot], 16 * loads)
            for n in range(2):
                k = 2 * j + n
                pe.wait_ge(s["silu"], k + 1)
                for c in range(2):
                    mm = pe.matmul(self.psG[:, :], self.W[:, slot, c * P:(c + 1) * P],
                                   self.src[:, c, n * 512:(n + 1) * 512], start=(c == 0), stop=(c == 1))
                mm.then_inc(s["gate"], 1)
                pe.wait_ge(s["mult"], k + 2)
                for c in range(2):
                    mm = pe.matmul(self.psU[:, :], self.W[:, slot, 256 + c * P:256 + (c + 1) * P],
                                   self.src[:, c, n * 512:(n + 1) * 512], start=(c == 0), stop=(c == 1))
                if self.spread:
                    sel, wT = self.spread
                    mm = pe.matmul(self.psB[:, :], sel[:, j * P:(j + 1) * P] if isinstance(j, int) else sel[:, ds(j * P, P)],
                                   wT[:, n * 512:(n + 1) * 512], start=True, stop=True)
                mm.then_inc(s["up"], 1)
            for n in range(2):
                pe.wait_ge(s["mult"], 2 * j + n + 3)
                if self.down is None:
                    rhs = self.W[:, slot, 512:768]
                else:
                    rhs = self.down[:, j, :] if isinstance(j, int) else self.down[:, ds(j, 1), :]
                for tt in range(4):
                    t = 4 * n + tt
                    out = self.acc[t // 2][:, (t % 2) * D:(t % 2 + 1) * D]
                    if self.down is not None and not isinstance(j, int):
                        out = out.unsqueeze(1)
                    mm = pe.matmul(out, self.h[:, n, tt * P:(tt + 1) * P], rhs,
                                   start=isinstance(j, int) and j == 0 and t % 2 == 0,
                                   stop=isinstance(j, int) and j == self.J - 1, skip_group_check=True)
                mm.then_inc(s["half"], 1)
        self.tiles(pe, body)

    def scalar(self, a):
        s = self.s
        a.sem_inc(s["silu"], 1)

        def body(j, slot, loads):
            for n in range(2):
                k = 2 * j + n
                a.wait_ge(s["gate"], k + 1)
                a.wait_ge(s["mult"], k + 1)
                if self.scales:
                    sc = self.scales[0][:, j:j + 1] if isinstance(j, int) else self.scales[0][:, ds(j, 1)]
                else:
                    sc = 1.0
                a.activation(self.sg[:, n, :], self.psG[:, :], ACT.Silu, scale=sc).then_inc(s["silu"], 1)
        self.tiles(a, body)

    def vector(self, v):
        s = self.s
        v.sem_inc(s["mult"], 2)

        def body(j, slot, loads):
            for n in range(2):
                k = 2 * j + n
                v.wait_ge(s["up"], k + 1)
                v.wait_ge(s["silu"], k + 2)
                v.wait_ge(s["half"], k + 3)
                h, sg = self.h[:, n, :], self.sg[:, n, :]
                if self.spread:
                    v.tensor_tensor(h, self.psU[:, :], sg, ALU.mult).then_inc(s["tmp"], 1)
                    v.wait_ge(s["tmp"], k + 1)
                    v.tensor_tensor(h, self.psB[:, :], h, ALU.mult).then_inc(s["mult"], 1)
                elif self.scales:
                    sc = self.scales[1][:, j:j + 1] if isinstance(j, int) else self.scales[1][:, ds(j, 1)]
                    v.scalar_tensor_tensor(out=h, in0=self.psU[:, :], scalar=sc, in1=sg, op0=ALU.mult,
                                           op1=ALU.mult).then_inc(s["mult"], 1)
                else:
                    v.tensor_tensor(h, self.psU[:, :], sg, ALU.mult).then_inc(s["mult"], 1)
        self.tiles(v, body)
        v.wait_ge(s["half"], 2 * self.J + 4)
        for t in range(NT):
            v.tensor_tensor(self.g.X[:, t, :], self.g.X[:, t, :], self.acc[t // 2][:, (t % 2) * D:(t % 2 + 1) * D],
                            ALU.add).then_inc(self.final, 1)
        v.wait_ge(self.final, NT)


def hadamard_ffn_stage(nc, g, stream, wscale_row):
    J, SC = 8, 64.0
    vec, wd = g.w["f0vec"], g.w["f0down"]
    with Stage(nc, "f0") as st:
        xs = st.sb("xs", [P, 2, TOK])
        hx = st.sb("hx", [P, 2, TOK])
        t1 = st.sb("t1", [P, J, D])
        t2 = st.sb("t2", [P, J, D])
        wrow = st.sb("wrow", [P, D])
        scl = st.sb("scl", [P, 2, J])
        ff = GatedFFN(g, st, J, stream, hx, resident_down=t2, scales=(scl[:, 0, :], scl[:, 1, :]))
        ln = LayerNorm(g, st, [ff.acc[0], ff.acc[1]])
        rowed, signed, mixed, wprod, wcopied, bfly, xprod, xcopied, scaled = st.sem(
            "row signed mixed wprod wcopied butterfly xprod xcopied scaled")
        with nc.Block() as block:
            @block.sync
            def _(sp):
                sp.dma_start(wrow[:, :], wscale_row.partition_broadcast(P)).then_inc(rowed, 16)
                ff.sync(sp)

            @block.gpsimd
            def _(p):
                ln.gpsimd(p)
                ln.wait(p)
                for c in range(2):
                    p.tensor_scalar(xs[:, c, :], g.xnT[:, c, :], vec[:, c:c + 1], None, ALU.mult).then_inc(signed, 1)
                p.wait_ge(signed, 2)
                p.tensor_tensor(g.xnT[:, 0, :], xs[:, 0, :], xs[:, 1, :], ALU.add).then_inc(mixed, 1)
                p.tensor_tensor(g.xnT[:, 1, :], xs[:, 0, :], xs[:, 1, :], ALU.subtract).then_inc(mixed, 1)

            @block.tensor
            def _(pe):
                for c in range(J):
                    if c % 2 == 0 and c >= 4:
                        pe.wait_ge(wcopied, c // 2 - 1)
                    bank = [ff.psG, ff.psU][c // 2 % 2]
                    mm = pe.matmul(bank[:, (c % 2) * D:(c % 2 + 1) * D], g.had, wd[:, c, :], start=True, stop=True)
                    if c % 2:
                        mm.then_inc(wprod, 1)
                ln.tensor(pe)
                pe.wait_ge(wcopied, 4)
                for c in range(2):
                    pe.wait_ge(mixed, c + 1)
                    for n in range(2):
                        k = 2 * c + n
                        if k >= 2:
                            pe.wait_ge(xcopied, k - 1)
                        pe.matmul([ff.psG, ff.psU][n][:, :], g.had, g.xnT[:, c, n * 512:(n + 1) * 512],
                                  start=True, stop=True).then_inc(xprod, 1)
                pe.wait_ge(xcopied, 4)
                ff.tensor(pe)

            @block.scalar
            def _(a):
                for k in range(4):
                    a.wait_ge(wprod, k + 1)
                    a.activation(t1[:, 2 * k:2 * k + 2, :], [ff.psG, ff.psU][k % 2][:, :].rearrange("p (c n) -> p c n", c=2),
                                 ACT.Copy).then_inc(wcopied, 1)
                ln.scalar(a)
                for k in range(4):
                    a.wait_ge(xprod, k + 1)
                    c, n = k // 2, k % 2
                    a.activation(hx[:, c, n * 512:(n + 1) * 512], [ff.psG, ff.psU][n][:, :], ACT.Copy,
                                 scale=1.0 / (16.0 * SC)).then_inc(xcopied, 1)
                a.wait_ge(scaled, 2)
                ff.scalar(a)

            @block.vector
            def _(v):
                v.tensor_scalar(scl[:, 0, :], vec[:, 18:26], SC, None, ALU.mult).then_inc(scaled, 1)
                v.scalar_tensor_tensor(out=scl[:, 1, :], in0=vec[:, 10:18], scalar=SC, in1=vec[:, 2:10],
                                       op0=ALU.mult, op1=ALU.mult).then_inc(scaled, 1)
                v.wait_ge(wcopied, 4)
                src, dst, n = t1, t2, 0
                for h in (1, 2, 4):
                    x = src[:, :, :].rearrange("p (a two h) n -> p a two (h n)", two=2, h=h)
                    y = dst[:, :, :].rearrange("p (a two h) n -> p a two (h n)", two=2, h=h)
                    v.tensor_tensor(y[:, :, 0, :], x[:, :, 0, :], x[:, :, 1, :], ALU.add).then_inc(bfly, 1)
                    v.tensor_tensor(y[:, :, 1, :], x[:, :, 0, :], x[:, :, 1, :], ALU.subtract).then_inc(bfly, 1)
                    n += 2
                    v.wait_ge(bfly, n)
                    src, dst = dst, src
                assert src is t2
                v.wait_ge(rowed, 16)
                v.scalar_tensor_tensor(out=t2[:, :, :], in0=t2[:, :, :], scalar=1.0 / 32.0,
                                       in1=wrow[:, :].unsqueeze(1).to_broadcast([P, J, D]), op0=ALU.mult,
                                       op1=ALU.mult).then_inc(bfly, 1)
                v.wait_ge(bfly, 7)
                ln.vector(v)
                ff.vector(v)


MH, MK, DCQ, MR = 16, 128, 192, 64
HQ = DCQ // 2
DOWN_AT = [4 * (2 * (n // 8) + n % 2) + (n // 2) % 4 for n in range(MH)]


def context_stage(nc, g, ins):
    with Stage(nc, "kv") as st:
        rT = st.sb("rT", [DC, B, LC])
        rK = st.sb("rK", [P, B, 2, DC])
        rL = st.sb("rL", [P, B, DC])
        tT = st.sb("tT", [DC, 2, LC])
        tK = st.sb("tK", [P, 2, 2, DC])
        tL = st.sb("tL", [P, 2, DC])
        gotT, gotK, gotL, turnT, turnK0, turnK1, turnL = \
            st.sem("gotT gotK gotL turnT turnK0 turnK1 turnL")
        with nc.Block() as block:
            @block.sync
            def _(sp):
                for dst, src, sem in ((g.KVT, "kvT", gotT), (rT, "kvTr", gotT), (tT, "tabT", gotT),
                                      (g.KVK, "kvK", gotK), (rK, "kvKr", gotK), (tK, "tabK", gotK)):
                    sp.dma_start(dst.ap(), ins[src]).then_inc(sem, 16)
                for dst, src in ((g.KVL, "kvL"), (rL, "kvLr"), (tL, "tabL")):
                    sp.dma_start(dst.ap().rearrange("p b d -> p (b d)"),
                                 ins[src].partition_broadcast(P)).then_inc(gotL, 16)

            def rope(eng, x, rot, cos, sin, done, n):
                eng.tensor_tensor(rot, rot, sin, ALU.mult).then_inc(done, 1)
                eng.tensor_tensor(x, x, cos, ALU.mult).then_inc(done, 1)
                eng.wait_ge(done, n + 2)
                eng.tensor_tensor(x, x, rot, ALU.add).then_inc(done, 1)

            def rope_keys(eng, c, done):
                rope(eng, g.KVK[:, :, c, :], rK[:, :, c, :], tK[:, 0:1, c, :].to_broadcast([P, B, DC]),
                     tK[:, 1:2, c, :].to_broadcast([P, B, DC]), done, 0)

            @block.vector
            def _(v):
                v.wait_ge(gotT, 48)
                rope(v, g.KVT[:, :, :], rT[:, :, :], tT[:, 0:1, :].to_broadcast([DC, B, LC]),
                     tT[:, 1:2, :].to_broadcast([DC, B, LC]), turnT, 0)
                v.wait_ge(gotK, 48)
                rope_keys(v, 1, turnK1)
                v.wait_ge(gotL, 48)
                rope(v, g.KVL[:, :, :], rL[:, :, :], tL[:, 0:1, :].to_broadcast([P, B, DC]),
                     tL[:, 1:2, :].to_broadcast([P, B, DC]), turnL, 0)

            @block.gpsimd
            def _(p):
                p.wait_ge(gotK, 48)
                rope_keys(p, 0, turnK0)


def fold_stage(nc, g, name, wide, narrow, Qm, Cm, Dm):
    join = Cm is None
    with Stage(nc, name) as st:
        W = st.sb("W", [P, 2, 256 + DCQ + DC + 256])
        R = st.sb("R", [MR, 2, DCQ + DC])
        AT = st.sb("AT", [HQ, 2, 2, 256])
        CS = st.sb("CS", [HQ, 2, 2, DC])
        psA = [st.ps(f"psA{u}", [P, 512]) for u in range(2)]
        psC = [st.ps(f"psC{u}", [P, 512]) for u in range(2)]
        psB = [st.ps(f"psB{u}", [P, 512]) for u in range(2)]
        psD = st.ps("psD", [P, 512])
        loaded = st.pair("loaded")
        ab, ca, cb, joined, kept, dd, dkept = st.sem("first firstA firstC joined kept down down_kept")
        with nc.Block() as block:
            @block.sync
            def _(sp):
                with sp.Fori(0, MH // 2) as i:
                    for u in range(2):
                        n = 2 * i + u
                        sp.wait_ge(dd, n + 1)
                        sp.dma_start(W[:, u, :], wide[ds(n, 1), :, :].rearrange("o p n -> (o p) n")).then_inc(loaded[u], 16)
                        sp.dma_start(R[:, u, :], narrow[ds(n, 1), :, :].rearrange("o p n -> (o p) n")).then_inc(loaded[u], 16)

            @block.tensor
            def _(pe):
                pe.sem_inc(dd, 2)
                with pe.Fori(0, MH // 2) as i:
                    for u in range(2):
                        n = 2 * i + u
                        pe.wait_ge(loaded[u], 32 * (i + 1))
                        pe.wait_ge(ca, n + 1)
                        pe.wait_ge(cb, n + 1)
                        for c in range(2):
                            if join:
                                pe.matmul(psA[u][0:HQ, c * 256:(c + 1) * 256], W[:, u, 256 + c * HQ:256 + (c + 1) * HQ],
                                          W[:, u, 0:256], start=True, stop=True)
                            else:
                                pe.matmul(psA[u][:, c * DCQ:(c + 1) * DCQ], W[:, u, c * P:(c + 1) * P],
                                          W[:, u, 256:256 + DCQ], start=True, stop=True)
                        for c in range(2):
                            mm = pe.matmul(psC[u][0:HQ, c * DC:(c + 1) * DC], R[:, u, c * HQ:(c + 1) * HQ],
                                           R[:, u, DCQ:DCQ + DC], start=True, stop=True)
                        mm.then_inc(ab, 1)
                        pe.wait_ge(dkept, i + 1)
                        pe.matmul(psD[u * DC:(u + 1) * DC, 0:256], W[:, u, 448:512], W[:, u, 512:768],
                                  start=True, stop=True).then_inc(dd, 1)
                        if join:
                            pe.wait_ge(ca, n + 3)
                            pe.wait_ge(cb, n + 3)
                            pe.wait_ge(kept, n + 1)
                            for k in range(2):
                                for c in range(2):
                                    mm = pe.matmul(psB[u][:, k * DC:(k + 1) * DC], AT[:, u, c, k * P:(k + 1) * P],
                                                   CS[:, u, c, :], start=(c == 0), stop=(c == 1))
                            mm.then_inc(joined, 1)

            @block.vector
            def _(v):
                v.sem_inc(ca, 2)
                v.sem_inc(cb, 2)
                v.sem_inc(kept, 2)
                v.sem_inc(dkept, 1)
                with v.Fori(0, MH // 2) as i:
                    for u in range(2):
                        n = 2 * i + u
                        v.wait_ge(ab, n + 1)
                        if join:
                            v.tensor_copy(AT[:, u, :, :], psA[u][0:HQ, 0:512].rearrange("p (c n) -> p c n", c=2)).then_inc(ca, 1)
                            v.tensor_copy(CS[:, u, :, :], psC[u][0:HQ, 0:2 * DC].rearrange("p (c n) -> p c n", c=2)).then_inc(cb, 1)
                            v.wait_ge(joined, n + 1)
                            v.tensor_scalar(Qm[:, :, ds(n * DC, DC)], psB[u][:, 0:2 * DC].rearrange("p (c n) -> p c n", c=2),
                                            1.0, None, ALU.mult).then_inc(kept, 1)
                        else:
                            v.tensor_scalar(Qm[:, :, ds(n * DCQ, DCQ)], psA[u][:, 0:2 * DCQ].rearrange("p (c n) -> p c n", c=2),
                                            1.0, None, ALU.mult).then_inc(ca, 1)
                            v.tensor_scalar(Cm[:, :, ds(n * DC, DC)], psC[u][0:HQ, 0:2 * DC].rearrange("p (c n) -> p c n", c=2),
                                            1.0, None, ALU.mult).then_inc(cb, 1)
                    v.wait_ge(dd, 2 * i + 4)
                    v.tensor_scalar(Dm[:, ds(i, 1), :], psD[:, 0:256].unsqueeze(1), 1.0, None, ALU.mult).then_inc(dkept, 1)


class LatentAttention:

    def __init__(self, g, st, Qm, Cm, Dm, rope):
        self.g, self.Qm, self.Cm, self.Dm, self.rope = g, Qm, Cm, Dm, rope
        self.QT = st.sb("QT", [DC, BT, MH, S])
        self.rt = st.sb("rt", [HQ, 2, 4, 512]) if rope is not None else None
        self.Pr = st.sb("Pr", [P, 2, 2, LC])
        self.PT = st.sb("PT", [P, 2, 4, P])
        self.nmx = st.sb("nmx", [P, 2, 2])
        self.sm = st.sb("sm", [P, 2, 4])
        self.ri = st.sb("ri", [P, 2, 4])
        self.CN = st.sb("CN", [P, 2, 4, DC])
        self.CT = st.sb("CT", [P, 8, P])
        self.psS = st.ps("psS", [P, 4, 512])
        self.psT = [st.ps(f"psT{n}", [P, 512]) for n in range(2)]
        self.psC = [st.ps(f"psC{n}", [P, 512]) for n in range(2)]
        self.s = {n: st.sem("m_" + n) for n in
                  "ab mul add cq qt sc mx ex tr pt pv last rin sum cn ct cte y added stood".split()}
        self.NQ = 4 if rope is not None else 2

    @staticmethod
    def staggered(eng, tile):
        QUERIES, UNITS, PROJECT = range(3)
        tile(0)[QUERIES]()
        with eng.Fori(0, NT - 1) as t:
            tile(t)[UNITS]()
            tile(t + 1)[QUERIES]()
            tile(t)[PROJECT]()
        tile(NT - 1)[UNITS]()
        tile(NT - 1)[PROJECT]()

    def tensor(self, pe):
        g, s, NQ = self.g, self.s, self.NQ
        def tile(t):
            def a_products(q):
                pe.wait_ge(s["ex"], 8 * t + 1) if q < 2 else pe.wait_ge(s["mul"], 4 * t + q - 1)
                for n in range(4):
                    for half in range(2):
                        for c in range(2):
                            at = (4 * q + n) * DCQ + half * HQ
                            mm = pe.matmul(self.psS[0:HQ, 2 * (q % 2) + half, n * P:(n + 1) * P],
                                           self.Qm[:, c, at:at + HQ], g.xnT[:, c, ds(t * P, P)],
                                           start=(c == 0), stop=(c == 1))
                mm.then_inc(s["ab"], 1)

            def c_products(q):
                pe.wait_ge(s["add"], 4 * t + q + 1)
                pe.wait_ge(s["pt"], 8 * t + 1) if q < 2 else pe.wait_ge(s["qt"], 4 * t + q - 1)
                for n in range(4):
                    for half in range(2):
                        at = (4 * q + n) * DC
                        mm = pe.matmul(self.psT[q % 2][0:DC, n * P:(n + 1) * P], self.Cm[:, half, at:at + DC],
                                       self.rt[:, q % 2, 2 * half, n * P:(n + 1) * P],
                                       start=(half == 0), stop=(half == 1))
                mm.then_inc(s["cq"], 1)

            def queries():
                if self.rope is not None:
                    for q in range(5):
                        if q < 4:
                            a_products(q)
                        if q >= 1:
                            c_products(q - 1)
                else:
                    pe.wait_ge(s["ex"], 8 * t + 1)
                    for k in range(2):
                        for n in range(4):
                            for c in range(2):
                                at = (4 * k + n) * P
                                mm = pe.matmul(self.psS[:, k, n * P:(n + 1) * P], self.Qm[:, c, at:at + P],
                                               g.xnT[:, c, ds(t * P, P)], start=(c == 0), stop=(c == 1))
                        mm.then_inc(s["cq"], 1)

            def scores(w):
                b, gp = w // 2, w % 2
                if w == 0:
                    pe.wait_ge(s["qt"], NQ * t + NQ)
                    if self.rope is not None:
                        pe.wait_ge(s["mul"], 4 * t + 4)
                if w >= 2:
                    pe.wait_ge(s["ex"], 8 * t + w)
                pe.sem_inc(s["stood"], 1)
                for r in range(2):
                    mm = pe.matmul(self.psS[:, 2 * (w % 2) + r, 0:LC].unsqueeze(1), self.QT[:, b, 4 * (2 * gp + r):4 * (2 * gp + r) + 4, :].rearrange("d n s -> d (n s)"),
                                   g.KVT[:, ds(4 * t + b, 1), :], start=True, stop=True)
                mm.then_inc(s["sc"], 1)

            def turn(w):
                pe.wait_ge(s["ex"], 8 * t + w + 2)
                if w >= 2:
                    pe.wait_ge(s["pt"], 8 * t + w)
                for r in range(2):
                    for c in range(2):
                        n = 2 * r + c
                        mm = pe.transpose(self.psT[w % 2][:, n * P:(n + 1) * P], self.Pr[:, w % 2, r, c * P:(c + 1) * P],
                                          g.ident[:, :])
                mm.then_inc(s["tr"], 1)

            def weigh(w):
                b, gp = w // 2, w % 2
                pe.wait_ge(s["pt"], 8 * t + w + 2)
                if w == 0:
                    pe.wait_ge(s["added"], t + 1)
                elif b >= 2 and gp == 0:
                    pe.wait_ge(s["cte"], 4 * t + b - 1)
                for r in range(2):
                    for c in range(2):
                        at = (2 * gp + r) * DC
                        mm = pe.matmul(self.psC[b % 2][:, at:at + DC].unsqueeze(1), self.PT[:, w % 2, 2 * r + c, :],
                                       g.KVK[:, ds(4 * t + b, 1), c, :], start=(c == 0), stop=(c == 1))
                mm.then_inc(s["pv"], 1)

            def turn_back(b):
                pe.wait_ge(s["cn"], 4 * t + b + 1)
                for gp in range(2):
                    mm = pe.transpose(self.psC[b % 2][:, 256 + gp * P:256 + (gp + 1) * P],
                                      self.CN[:, b % 2, 2 * gp:2 * gp + 2, :].rearrange("p r d -> p (r d)"), g.ident[:, :])
                mm.then_inc(s["ct"], 1)

            def units():
                scores(0)
                for w in range(8):
                    if w < 7:
                        scores(w + 1)
                    turn(w)
                    if w >= 1:
                        weigh(w - 1)
                    if w >= 3 and w % 2:
                        turn_back((w - 3) // 2)
                weigh(7)

            def project():
                turn_back(3)
                pe.wait_ge(s["cte"], 4 * t + 4)
                for n in range(8):
                    mm = pe.matmul(self.psC[0][:, 0:D], self.CT[:, n, :], self.Dm[:, n, :], start=(n == 0), stop=(n == 7))
                mm.then_inc(s["y"], 1)

            return queries, units, project

        self.staggered(pe, tile)

    def gpsimd(self, p):
        if self.rope is None:
            return
        s = self.s
        with p.Fori(0, NT) as t:
            for q in range(4):
                p.wait_ge(s["mul"], 4 * t + q + 1)
                r = self.rt[:, q % 2, :, :]
                p.tensor_tensor(r[:, 0, :], r[:, 0, :], r[:, 1, :], ALU.subtract)
                p.tensor_tensor(r[:, 2, :], r[:, 2, :], r[:, 3, :], ALU.add).then_inc(s["add"], 1)

    def scalar(self, a):
        s, NQ = self.s, self.NQ
        a.sem_inc(s["ex"], 1)
        a.sem_inc(s["pt"], 1)
        def tile(t):
            def queries():
                if self.rope is not None:
                    for q in range(4):
                        a.wait_ge(s["cq"], 4 * t + q + 1)
                        a.activation(self.QT[:, :, 4 * q:4 * q + 4, :].rearrange("d b n s -> d n b s"),
                                     self.psT[q % 2][0:DC, :].rearrange("d (n b s) -> d n b s", n=4, b=BT),
                                     ACT.Copy).then_inc(s["qt"], 1)
                else:
                    for k in range(2):
                        a.wait_ge(s["cq"], 2 * t + k + 1)
                        for r in range(2):
                            ins = a.activation(self.QT[:, :, 8 * k + r:8 * k + 8:2, :].rearrange("d b n s -> d n b s"),
                                               self.psS[r * DC:(r + 1) * DC, k, :].rearrange("d (n b s) -> d n b s", n=4, b=BT),
                                               ACT.Copy)
                        ins.then_inc(s["qt"], 1)

            def exps(w):
                b, gp = w // 2, w % 2
                a.wait_ge(s["mx"], 8 * t + w + 1)
                if w >= 2:
                    a.wait_ge(s["tr"], 8 * t + w - 1)
                    a.wait_ge(s["last"], 4 * t + b)
                for r in range(2):
                    ins = a.activation(self.Pr[:, gp, r, :], self.psS[:, 2 * gp + r, 0:LC], ACT.Exp,
                                       bias=self.nmx[:, gp, r:r + 1], accum_out=self.sm[:, b % 2, 2 * gp + r:2 * gp + r + 1])
                ins.then_inc(s["ex"], 1)

            def keep(w):
                a.wait_ge(s["tr"], 8 * t + w + 1)
                if w >= 2:
                    a.wait_ge(s["pv"], 8 * t + w - 1)
                a.activation(self.PT[:, w % 2, :, :].rearrange("p n k -> p (n k)"), self.psT[w % 2][:, :],
                             ACT.Copy).then_inc(s["pt"], 1)

            def keep_back(b):
                a.wait_ge(s["ct"], 4 * t + b + 1)
                a.activation(self.CT[:, :, b * S:(b + 1) * S],
                             self.psC[b % 2][:, 256:512].rearrange("p (n s) -> p n s", s=S), ACT.Copy).then_inc(s["cte"], 1)

            def units():
                exps(0)
                for w in range(8):
                    if w < 7:
                        exps(w + 1)
                    keep(w)
                    if w >= 3 and w % 2:
                        keep_back((w - 3) // 2)

            return queries, units, lambda: keep_back(3)

        self.staggered(a, tile)

    def vector(self, v):
        g, s = self.g, self.s
        v.sem_inc(s["added"], 1)
        def tile(t):
            def queries():
                if self.rope is None:
                    return
                def tab(f, half):
                    return self.rope[0:HQ, f, half:half + 1, :].to_broadcast([HQ, 16, S])
                for q in range(4):
                    v.wait_ge(s["ab"], 4 * t + q + 1)
                    if q >= 2:
                        v.wait_ge(s["cq"], 4 * t + q - 1)
                    for n, (src, f, half) in enumerate(((0, 0, 0), (1, 1, 0), (1, 0, 1), (0, 1, 1))):
                        ins = v.tensor_tensor(self.rt[:, q % 2, n, :].rearrange("p (k s) -> p k s", s=S),
                                              self.psS[0:HQ, 2 * (q % 2) + src, :].rearrange("p (k s) -> p k s", s=S),
                                              tab(f, half), ALU.mult)
                    ins.then_inc(s["mul"], 1)

            def maxes(w):
                v.wait_ge(s["sc"], 8 * t + w + 1)
                v.wait_ge(s["ex"], 8 * t + max(w, 1))
                v.tensor_reduce(self.nmx[:, w % 2, :], self.psS[:, 2 * (w % 2):2 * (w % 2) + 2, 0:LC], AXX, ALU.max,
                                negate=True).then_inc(s["mx"], 1)

            def last_key(b):
                cn = self.CN[:, b % 2, :, :]
                v.wait_ge(s["ex"], 8 * t + 2 * b + 3)
                if b >= 2:
                    v.wait_ge(s["ct"], 4 * t + b - 1)
                v.tensor_tensor(cn, g.KVL[:, ds(4 * t + b, 1), :].to_broadcast([P, 4, DC]),
                                self.Pr[:, :, :, LC - 1:LC].rearrange("p a r o -> p (a r) o").to_broadcast([P, 4, DC]),
                                ALU.mult).then_inc(s["last"], 1)
                v.reciprocal(self.ri[:, b % 2, :], self.sm[:, b % 2, :]).then_inc(s["rin"], 1)

            def finish(b):
                cn = self.CN[:, b % 2, :, :]
                v.wait_ge(s["last"], 4 * t + b + 1)
                v.wait_ge(s["pv"], 8 * t + 2 * b + 2)
                v.tensor_tensor(cn, self.psC[b % 2][:, 0:4 * DC].rearrange("p (n d) -> p n d", n=4), cn,
                                ALU.add).then_inc(s["sum"], 1)
                v.wait_ge(s["sum"], 4 * t + b + 1)
                v.wait_ge(s["rin"], 4 * t + b + 1)
                v.tensor_tensor(cn, cn, self.ri[:, b % 2, :].unsqueeze(2).to_broadcast([P, 4, DC]),
                                ALU.mult).then_inc(s["cn"], 1)

            def units():
                maxes(0)
                maxes(1)
                for w in range(2, 8):
                    maxes(w)
                    if w % 2:
                        finish((w - 3) // 2)
                    else:
                        last_key((w - 2) // 2)
                last_key(3)
                finish(3)

            def project():
                v.wait_ge(s["y"], t + 1)
                x = g.X[:, ds(t, 1), :]
                v.tensor_tensor(x, x, self.psC[0][:, 0:D].unsqueeze(1), ALU.add).then_inc(s["added"], 1)

            return queries, units, project

        self.staggered(v, tile)


def latent_stage(nc, g, name, Qm, Cm, Dm, rope):
    with Stage(nc, name) as st:
        at = LatentAttention(g, st, Qm, Cm, Dm, rope)
        ln = LayerNorm(g, st, [at.psT[0], at.psT[1]])
        with nc.Block() as block:
            @block.vector
            def _(v):
                ln.vector(v)
                at.vector(v)

            @block.gpsimd
            def _(p):
                ln.gpsimd(p)
                at.gpsimd(p)

            @block.tensor
            def _(pe):
                ln.tensor(pe)
                ln.wait(pe)
                at.tensor(pe)

            @block.scalar
            def _(a):
                ln.scalar(a)
                at.scalar(a)


def similarity_stage(nc, g, scratch):
    w1, w2, w3, vec = g.w["s1w1"], g.w["s1w2"], g.w["s1w3"], g.w["s1vec"]
    KEEP, TAKEN = 3, -3.0e38
    with Stage(nc, "s1") as st:
        x0 = st.sb("x0", [P, NT, D])
        hT = st.sb("hT", [P, TOK])
        pair = st.sb("pair", [P, 2, S, S])
        g2 = st.sb("g2", [P, 2, 512])
        sim8 = st.sb("sim8", [2 * BT, NT, 512])
        sim = st.sb("sim", [P, NT, S])
        left = st.sb("left", [P, NT, S])
        top = st.sb("top", [P, NT, 8])
        ps2 = [st.ps(f"ps2{n}", [P, 512]) for n in range(2)]
        ps3 = st.ps("ps3", [P, 512])
        psH = [st.ps(f"psH{n}", [P, 512]) for n in range(2)]
        lna = LayerNorm(g, st, None, keep=x0, pre="a")
        lnb = LayerNorm(g, st, psH, src=x0, affine=vec, pre="b")
        resid, hp, hk, dif, rel, mid, midk, last, simk, wrote, read, ranked = st.sem(
            "residual h_product h_kept pairs relu middle middle_kept last sim_kept wrote read ranked")
        with nc.Block() as block:
            @block.gpsimd
            def _(p):
                lna.gpsimd(p)
                for u in range(2):
                    p.wait_ge(lna.normed[u], NT // 2)
                p.tensor_tensor(g.X[:, :, :], g.X[:, :, :], x0[:, :, :], ALU.add).then_inc(resid, 1)
                lnb.gpsimd(p)

            @block.tensor
            def _(pe):
                lnb.tensor(pe)
                lnb.wait(pe)
                for n in range(2):
                    for c in range(2):
                        mm = pe.matmul(psH[n][:, :], w1[:, c, :], g.xnT[:, c, n * 512:(n + 1) * 512],
                                       start=(c == 0), stop=(c == 1))
                    mm.then_inc(hp, 1)
                with pe.Fori(0, NT) as t:
                    def middle(b):
                        pe.wait_ge(rel, BT * t + b + 1)
                        pe.wait_ge(midk, BT * t + b + 1)
                        for ih in range(2):
                            mm = pe.matmul(ps2[b % 2][ih * 64:(ih + 1) * 64, :], w2[:, :],
                                           pair[:, b % 2, ih * 16:(ih + 1) * 16, :].rearrange("p i j -> p (i j)"),
                                           start=True, stop=True)
                        mm.then_inc(mid, 1)

                    def third(b):
                        pe.wait_ge(midk, BT * t + b + 3)
                        if b == 0:
                            pe.wait_ge(simk, t + 1)
                        pe.matmul(ps3[0:2 * BT, :], w3[:, b, :], g2[:, b % 2, :], start=(b == 0),
                                  stop=(b == BT - 1)).then_inc(last, 1)

                    middle(0)
                    for b in range(1, BT):
                        middle(b)
                        third(b - 1)
                    third(BT - 1)

            @block.scalar
            def _(a):
                lnb.scalar(a)
                for n in range(2):
                    a.wait_ge(hp, n + 1)
                    a.activation(hT[:, n * 512:(n + 1) * 512], psH[n][:, :], ACT.Copy).then_inc(hk, 1)
                a.sem_inc(midk, 2)
                with a.Fori(0, NT) as t:
                    def relu1(b):
                        a.wait_ge(dif, BT * t + b + 1)
                        x = pair[:, b % 2, :, :].rearrange("p i j -> p (i j)")
                        a.activation(x, x, ACT.Relu, bias=vec[:, 4:5]).then_inc(rel, 1)

                    def relu2(b):
                        a.wait_ge(mid, BT * t + b + 1)
                        if b >= 2:
                            a.wait_ge(last, BT * t + b - 1)
                        a.activation(g2[:, b % 2, :], ps2[b % 2][:, :], ACT.Relu, bias=vec[:, 5:6]).then_inc(midk, 1)

                    relu1(0)
                    for b in range(1, BT):
                        relu1(b)
                        relu2(b - 1)
                    relu2(BT - 1)

            @block.vector
            def _(v):
                lna.vector(v)
                for u in range(2):
                    v.wait_ge(lna.normed[u], NT // 2)
                lnb.vector(v)
                v.wait_ge(hk, 2)
                v.sem_inc(simk, 1)
                with v.Fori(0, NT) as t:
                    for b in range(BT):
                        h = hT[:, ds(t * P + b * S, S)]
                        if b >= 2:
                            v.wait_ge(mid, BT * t + b - 1)
                        v.tensor_tensor(pair[:, b % 2, :, :], h.unsqueeze(2).to_broadcast([P, S, S]),
                                        h.unsqueeze(1).to_broadcast([P, S, S]), ALU.subtract).then_inc(dif, 1)
                    v.wait_ge(last, BT * t + BT)
                    v.tensor_scalar(sim8[:, ds(t, 1), :], ps3[0:2 * BT, :].unsqueeze(1), vec[0:2 * BT, 6:7], None,
                                    ALU.add).then_inc(simk, 1)
                v.wait_ge(read, 16)
                v.tensor_tensor(sim[:, :, :], sim[:, :, :], g.offdiag.unsqueeze(1).to_broadcast([P, NT, S]),
                                ALU.mult).then_inc(ranked, 1)
                v.wait_ge(ranked, 1)
                for t in range(NT):
                    v.max(top[:, t, :], sim[:, t, :]).then_inc(ranked, 1)
                v.wait_ge(ranked, 1 + NT)
                v.memset(top[:, :, KEEP:8], -TAKEN).then_inc(ranked, 1)
                v.wait_ge(ranked, 2 + NT)
                for t in range(NT):
                    v.match_replace(out=left[:, t, :], in_to_replace=top[:, t, :], in_values=sim[:, t, :],
                                    imm_value=TAKEN).then_inc(ranked, 1)
                v.wait_ge(ranked, 2 + 2 * NT)
                v.tensor_scalar(left[:, :, :], left[:, :, :], TAKEN, -1.0, ALU.is_equal, ALU.add).then_inc(ranked, 1)
                v.wait_ge(ranked, 3 + 2 * NT)
                v.tensor_scalar(g.KM[:, :, :], left[:, :, :], -NEG, None, ALU.mult).then_inc(ranked, 1)

            @block.sync
            def _(sp):
                sp.wait_ge(simk, NT + 1)
                sp.dma_start(scratch.rearrange("t r n -> r t n"), sim8[:, :, :]).then_inc(wrote, 16)
                sp.wait_ge(wrote, 16)
                sp.dma_start(sim[:, :, :], scratch.rearrange("t r (i j) -> (r i) t j", j=S)).then_inc(read, 16)
                sp.wait_ge(read, 16)


class Router:

    def __init__(self, g, st, banks, E, wr, top_p=None, top_k=None, shared=False):
        self.g, self.E, self.wr, self.top_p, self.top_k, self.shared = g, E, wr, top_p, top_k, shared
        self.p = st.sb("rp", [P, NT, E])
        self.mx = st.sb("rmx", [P, NT])
        self.cmp = st.sb("rcmp", [P, NT, E, E])
        self.eq = st.sb("req", [P, NT, E, E])
        self.ex = st.sb("rex", [P, NT, E])
        self.rest = st.sb("rrest", [P, NT, E])
        self.parts = st.sb("rparts", [P, NT, 96], BF16)
        self.wT = st.sb("rwT", [96, TOK], BF16)
        self.psR = banks[0][:, 0:NT * E]
        self.psW = banks[1]
        self.logit, self.chain, self.shifted, self.exped, self.split, self.turned, self.ready = st.sem(
            "r_logit r_chain r_shifted r_exped r_split r_turned r_ready")

    def tensor(self, pe):
        for t in range(NT):
            for c in range(2):
                mm = pe.matmul(self.psR[:, t * self.E:(t + 1) * self.E], self.g.xnT[:, c, t * P:(t + 1) * P],
                               self.wr[:, c, :], start=(c == 0), stop=(c == 1))
        mm.then_inc(self.logit, 1)
        pe.wait_ge(self.split, 1)
        for t in range(NT):
            mm = pe.transpose(self.psW[:, t * P:(t + 1) * P], self.parts[:, t, :], self.g.identb[:, :])
        mm.then_inc(self.turned, 1)

    def scalar(self, a):
        a.wait_ge(self.shifted, 1)
        a.activation(self.p[:, :, :], self.p[:, :, :], ACT.Exp).then_inc(self.exped, 1)
        a.wait_ge(self.turned, 1)
        a.activation(self.wT[:, :], self.psW[:, :], ACT.Copy).then_inc(self.ready, 1)

    def vector(self, v):
        E, p, n = self.E, self.p, [0]

        def link(ins):
            ins.then_inc(self.chain, 1)
            n[0] += 1
            v.wait_ge(self.chain, n[0])

        def wide(x):
            return x.unsqueeze(2).to_broadcast([P, NT, E])

        link(v.memset(self.parts[:, :, :], 0.0))
        v.wait_ge(self.logit, 1)
        logits = self.psR[:, :].rearrange("p (t e) -> p t e", t=NT)
        link(v.tensor_reduce(self.mx[:, :], logits, AXX, ALU.max))
        v.tensor_tensor(p[:, :, :], logits, wide(self.mx[:, :]), ALU.subtract).then_inc(self.shifted, 1)
        v.wait_ge(self.exped, 1)
        link(v.tensor_reduce(self.mx[:, :], p[:, :, :], AXX, ALU.add))
        link(v.reciprocal(self.mx[:, :], self.mx[:, :]))
        link(v.tensor_tensor(p[:, :, :], p[:, :, :], wide(self.mx[:, :]), ALU.mult))
        pk = p[:, :, :].unsqueeze(2).to_broadcast([P, NT, E, E])
        pj = p[:, :, :].unsqueeze(3).to_broadcast([P, NT, E, E])
        link(v.tensor_tensor(self.cmp[:, :, :, :], pk, pj, ALU.is_gt))
        link(v.tensor_tensor(self.eq[:, :, :, :], pk, pj, ALU.is_equal))
        early = self.g.earlier[:, :].rearrange("p (j k) -> p j k", j=16)[:, 0:E, 0:E].unsqueeze(1).to_broadcast([P, NT, E, E])
        link(v.tensor_tensor(self.eq[:, :, :, :], self.eq[:, :, :, :], early, ALU.mult))
        link(v.tensor_tensor(self.cmp[:, :, :, :], self.cmp[:, :, :, :], self.eq[:, :, :, :], ALU.add))
        if self.top_p is not None:
            link(v.tensor_tensor(self.cmp[:, :, :, :], self.cmp[:, :, :, :], pk, ALU.mult))
            link(v.tensor_reduce(self.ex[:, :, :], self.cmp[:, :, :, :], AXX, ALU.add))
            link(v.tensor_scalar(self.ex[:, :, :], self.ex[:, :, :], self.top_p, None, ALU.is_le))
            link(v.tensor_tensor(p[:, :, :], p[:, :, :], self.ex[:, :, :], ALU.mult))
        else:
            link(v.tensor_reduce(self.ex[:, :, :], self.cmp[:, :, :, :], AXX, ALU.add))
            link(v.tensor_scalar(self.ex[:, :, :], self.ex[:, :, :], self.top_k - 0.5, None, ALU.is_lt))
            link(v.tensor_tensor(p[:, :, :], p[:, :, :], self.ex[:, :, :], ALU.mult))
            link(v.tensor_reduce(self.mx[:, :], p[:, :, :], AXX, ALU.add))
            link(v.tensor_scalar(self.mx[:, :], self.mx[:, :], 1e-20, None, ALU.add))
            link(v.reciprocal(self.mx[:, :], self.mx[:, :]))
            link(v.tensor_tensor(p[:, :, :], p[:, :, :], wide(self.mx[:, :]), ALU.mult))
        src, dst = p, self.rest
        for k in range(3):
            part = self.parts[:, :, 32 * k:32 * k + E]
            ins = v.tensor_copy(part, src[:, :, :])
            if k < 2:
                link(ins)
                link(v.tensor_tensor(dst[:, :, :], src[:, :, :], part, ALU.subtract))
                src, dst = dst, src
            else:
                link(ins)
        if self.shared:
            link(v.memset(self.parts[:, :, E:E + 1], 1.0))
        v.sem_inc(self.split, 1)


def experts_stage(nc, g, name, J, stream, selection, E, wr, top_p=None, top_k=None, shared=False):
    with Stage(nc, name) as st:
        sel = st.sb("sel", [96, J * P], BF16)
        psW = st.ps("psW", [96, TOK], BF16)
        ff = GatedFFN(g, st, J, stream, g.xnT, spread=(sel, None))
        rt = Router(g, st, [ff.psG, psW], E, wr, top_p, top_k, shared)
        ff.spread = (sel, rt.wT)
        ln = LayerNorm(g, st, [ff.acc[0], ff.acc[1]])
        selected = st.sem("selected")
        with nc.Block() as block:
            @block.sync
            def _(sp):
                sp.dma_start(sel[:, :], selection).then_inc(selected, 16)
                ff.sync(sp)

            @block.gpsimd
            def _(p):
                ln.gpsimd(p)

            @block.tensor
            def _(pe):
                ln.tensor(pe)
                ln.wait(pe)
                rt.tensor(pe)
                pe.wait_ge(rt.ready, 1)
                pe.wait_ge(selected, 16)
                ff.tensor(pe)

            @block.scalar
            def _(a):
                ln.scalar(a)
                rt.scalar(a)
                ff.scalar(a)

            @block.vector
            def _(v):
                ln.vector(v)
                rt.vector(v)
                ff.vector(v)


def normed_memory_stage(nc, g):
    win, wg, wout, vec = g.w["m2in"], g.w["m2gate"], g.w["m2out"], g.w["m2vec"]
    EPS = 1e-6
    with Stage(nc, "m2") as st:
        xp = st.sb("xp", [P, 2, TOK])
        IG, FG, OG, CG = [st.sb(n, [P, 2, TOK]) for n in ("ig", "fg", "og", "cg")]
        CS = st.sb("cs", [P, 2, TOK])
        ps = [st.ps(f"gate{n}", [P, 512]) for n in range(4)]
        pst = [st.ps(f"out{n}", [P, 512]) for n in range(2)]
        ln = LayerNorm(g, st, pst)
        xprod, xkept, gated, opened, fed, reset, scanned, squared, meaned, eased, rooted, inverse, normed, tanhed, hid, \
            prod, added = st.sem("xprod xkept gated opened fed reset scanned squared meaned eased rooted inverse "
                                 "normed tanhed hidden product added")
        order = ((0, IG, ACT.Exp), (3, CG, ACT.Tanh), (1, FG, ACT.Sigmoid), (2, OG, ACT.Sigmoid))
        groups = [(gate, m, n) for gate in range(4) for m in range(2) for n in range(2)]
        with nc.Block() as block:
            @block.tensor
            def _(pe):
                ln.tensor(pe)
                ln.wait(pe)
                for m in range(2):
                    for n in range(2):
                        for c in range(2):
                            mm = pe.matmul(ps[2 * m + n][:, :], win[:, c, m * P:(m + 1) * P],
                                           g.xnT[:, c, n * 512:(n + 1) * 512], start=(c == 0), stop=(c == 1))
                        mm.then_inc(xprod, 1)
                pe.wait_ge(xkept, 4)
                for k, (gate, m, n) in enumerate(groups):
                    if k >= 4:
                        pe.wait_ge(opened, k - 3)
                    for c in range(2):
                        at = order[gate][0] * 256 + m * P
                        mm = pe.matmul(ps[k % 4][:, :], wg[:, c, at:at + P], xp[:, c, n * 512:(n + 1) * 512],
                                       start=(c == 0), stop=(c == 1))
                    mm.then_inc(gated, 1)
                pe.wait_ge(opened, 16)
                for m in range(2):
                    pe.wait_ge(squared, m + 1)
                    for n in range(2):
                        pe.matmul(ps[2 * m + n][:, :], g.headmean, IG[:, m, n * 512:(n + 1) * 512], start=True,
                                  stop=True).then_inc(meaned, 1)
                pe.wait_ge(hid, 2)
                for t in range(NT):
                    if t >= 2:
                        pe.wait_ge(added, t - 1)
                    for c in range(2):
                        mm = pe.matmul(pst[t % 2][:, 0:D], OG[:, c, t * P:(t + 1) * P], wout[:, c, :],
                                       start=(c == 0), stop=(c == 1))
                    mm.then_inc(prod, 1)

            @block.scalar
            def _(a):
                ln.scalar(a)
                for k in range(4):
                    a.wait_ge(xprod, k + 1)
                    a.activation(xp[:, k // 2, (k % 2) * 512:(k % 2 + 1) * 512], ps[k][:, :], ACT.Copy).then_inc(xkept, 1)
                for k, (gate, m, n) in enumerate(groups):
                    a.wait_ge(gated, k + 1)
                    col = 2 * order[gate][0] + m
                    a.activation(order[gate][1][:, m, n * 512:(n + 1) * 512], ps[k % 4][:, :], order[gate][2],
                                 bias=vec[:, col:col + 1]).then_inc(opened, 1)
                for m in range(2):
                    a.wait_ge(eased, 2 * m + 2)
                    a.activation(CG[:, m, :], CG[:, m, :], ACT.Sqrt).then_inc(rooted, 1)
                for m in range(2):
                    a.wait_ge(normed, m + 1)
                    a.activation(CS[:, m, :], CS[:, m, :], ACT.Tanh).then_inc(tanhed, 1)

            @block.gpsimd
            def _(p):
                ln.gpsimd(p)
                for m in range(2):
                    p.wait_ge(opened, 6 + 2 * m)
                    p.tensor_tensor(CG[:, m, :], CG[:, m, :], IG[:, m, :], ALU.mult).then_inc(fed, 1)
                for m in range(2):
                    p.wait_ge(scanned, m + 1)
                    p.tensor_tensor(IG[:, m, :], CS[:, m, :], CS[:, m, :], ALU.mult).then_inc(squared, 1)
                for m in range(2):
                    p.wait_ge(tanhed, m + 1)
                    p.tensor_tensor(OG[:, m, :], OG[:, m, :], CS[:, m, :], ALU.mult).then_inc(hid, 1)

            @block.vector
            def _(v):
                ln.vector(v)
                for m in range(2):
                    v.wait_ge(opened, 10 + 2 * m)
                    v.memset(FG[:, m, :].rearrange("p (b s) -> p b s", s=S)[:, :, 0:1], 0.0).then_inc(reset, 1)
                    v.wait_ge(reset, m + 1)
                    v.wait_ge(fed, m + 1)
                    v.tensor_tensor_scan(CS[:, m, :], FG[:, m, :], CG[:, m, :], 0.0, ALU.mult, ALU.add).then_inc(scanned, 1)
                v.wait_ge(scanned, 2)
                for k in range(4):
                    v.wait_ge(meaned, k + 1)
                    v.tensor_scalar(CG[:, k // 2, (k % 2) * 512:(k % 2 + 1) * 512], ps[k][:, :], EPS, None,
                                    ALU.add).then_inc(eased, 1)
                for m in range(2):
                    v.wait_ge(rooted, m + 1)
                    v.reciprocal(CG[:, m, :], CG[:, m, :]).then_inc(inverse, 1)
                    v.wait_ge(inverse, m + 1)
                    v.wait_ge(squared, m + 1)
                    v.scalar_tensor_tensor(out=CS[:, m, :], in0=CS[:, m, :], scalar=vec[:, 8:9], in1=CG[:, m, :],
                                           op0=ALU.mult, op1=ALU.mult).then_inc(normed, 1)
                for t in range(NT):
                    v.wait_ge(prod, t + 1)
                    v.tensor_tensor(g.X[:, t, :], g.X[:, t, :], pst[t % 2][:, 0:D], ALU.add).then_inc(added, 1)


class Chain:

    def __init__(self, eng, sem, per, rnd):
        self.eng, self.sem, self.per, self.rnd, self.n = eng, sem, per, rnd, 0

    def link(self, ins):
        ins.then_inc(self.sem, 1)
        self.n += 1
        self.eng.wait_ge(self.sem, self.rnd * self.per + self.n)


def quantised_ffn_stage(nc, g, ins):
    QB, MAGIC, EPS, HID = 127.0, 12582912.0, 1e-5, 1024
    with Stage(nc, "q3") as st:
        wgv, wo = st.sb("wgv", [P, 2, 2 * HID]), st.sb("wo", [P, 8, D])
        tgv, tos = st.sb("tgv", [P, 2, 2 * HID], BF16), st.sb("tos", [P, 8, D], BF16)
        below = st.sb("below", [P, 2 * 2 * HID], BF16)
        nw = st.sb("nw", [P, D])
        xn = st.sb("xn", [P, NT, D])
        sq = st.sb("sq", [P, D])
        ss, rr = st.sb("ss", [P, NT]), st.sb("rr", [P, NT])
        ws = st.sb("ws", [P, 2, 4])
        h = st.sb("h", [P, NT, D])
        hr = st.sb("hr", [P, HID])
        hv, sg = st.sb("hv", [P, HID]), st.sb("sg", [P, HID])
        hq, vq = st.sb("hq", [P, NT, D], BF16), st.sb("vq", [P, HID], BF16)
        qT, vT = st.sb("qT", [P, NT * 2, P], BF16), st.sb("vT", [P, 8, P], BF16)
        hmax, hinv, hback = st.sb("hmax", [P, NT]), st.sb("hinv", [P, NT]), st.sb("hback", [P, NT])
        am = st.sb("am", [P, 2])
        vback = st.sb("vback", [P, NT])
        psV = st.ps("psV", [P, HID])
        psG = st.ps("psG", [P, HID])
        psQ, psW = st.ps("psQ", [P, 8 * P], BF16), st.ps("psW", [P, 8 * P], BF16)
        psY, psM = st.ps("psY", [P, 512]), st.ps("psM", [P, 512])
        ln = LayerNorm(g, st, None, keep=xn)
        wl, nl, wsum, wmean, wchain, squares, eased, powd, resid, hchain, chain, quant, qt, qk, gp, vp, silu, \
            vquant, vt, vk, y, added, backs, stood = \
            st.sem("w_loaded nw_loaded w_sum w_mean w_chain squares eased powered residual h_chain chain quantised "
                   "turned turned_kept gates values silu v_quantised v_turned v_kept y added backs stood")
        read = lambda t: 7 * t + 1
        with nc.Block() as block:
            @block.sync
            def _(sp):
                sp.dma_start(wgv.ap(), ins["q3gv"]).then_inc(wl, 16)
                sp.dma_start(wo.ap(), ins["q3out"]).then_inc(wl, 16)
                sp.dma_start(nw[:, :], ins["q3norm"].partition_broadcast(P)).then_inc(nl, 16)

            @block.gpsimd
            def _(p):
                ln.gpsimd(p)
                for u in range(2):
                    p.wait_ge(ln.normed[u], NT // 2)
                p.tensor_tensor(g.X[:, :, :], g.X[:, :, :], xn[:, :, :], ALU.add).then_inc(resid, 1)
                p.wait_ge(eased, 1)
                p.tensor_tensor(rr[:, :], ss[:, :], g.mhalf[:, 0:NT], ALU.pow).then_inc(powd, 1)

            @block.tensor
            def _(pe):
                pe.wait_ge(wsum, 2)
                pe.matmul(psM[:, 0:2], g.ones, ws[:, :, 0], start=True, stop=True).then_inc(wmean, 1)
                pe.wait_ge(wchain, W_STEPS)
                pe.wait_ge(quant, 1)
                for half, bank in enumerate((psQ, psW)):
                    for n in range(8):
                        t, c = divmod(half * 8 + n, 2)
                        mm = pe.transpose(bank[:, n * P:(n + 1) * P], hq[:, t, c * P:(c + 1) * P], g.identb[:, :])
                    mm.then_inc(qt, 1)

                def gates(t):
                    for part, (bank, sem) in enumerate(((psV, vp), (psG, gp))):
                        for n in range(2):
                            for c in range(2):
                                at = part * HID + n * 512
                                mm = pe.matmul(bank[:, n * 512:(n + 1) * 512], turned(t, c), tgv[:, c, at:at + 512],
                                               start=(c == 0), stop=(c == 1))
                        mm.then_inc(sem, 1)

                def turned(t, c):
                    if isinstance(t, int):
                        return qT[:, 2 * t + c, :]
                    return qT[:, ds(2 * t + c, 1), :].squeeze(1)

                def down(t, first=False):
                    pe.wait_ge(vquant, t + 1)
                    for c in range(8):
                        mm = pe.transpose(psW[:, c * P:(c + 1) * P], vq[:, c * P:(c + 1) * P], g.identb[:, :])
                    mm.then_inc(vt, 1)
                    pe.wait_ge(vk, t + 1)
                    pe.wait_ge(added, t + 1)
                    for c in range(8):
                        mm = pe.matmul(psY[:, 0:D], vT[:, c, :], tos[:, c, :], start=(c == 0), stop=(c == 7))
                    mm.then_inc(y, 1)

                pe.wait_ge(qk, 2)
                gates(0)
                with pe.Fori(0, NT - 1) as t:
                    pe.wait_ge(chain, read(t))
                    gates(t + 1)
                    down(t)
                down(NT - 1)

            @block.scalar
            def _(a):
                for u in range(2):
                    a.wait_ge(ln.normed[u], NT // 2)
                for t in range(NT):
                    if t:
                        a.wait_ge(squares, t)
                    a.activation(sq[:, :], xn[:, t, :], ACT.Square, accum_out=ss[:, t:t + 1]).then_inc(squares, 1)
                for half, bank in enumerate((psQ, psW)):
                    a.wait_ge(qt, half + 1)
                    a.activation(qT[:, 8 * half:8 * half + 8, :].rearrange("p c n -> p (c n)"), bank[:, :],
                                 ACT.Copy).then_inc(qk, 1)

                def silu_of(scale, t):
                    a.wait_ge(gp, t + 1)
                    a.sem_inc(stood, 1)
                    a.activation(sg[:, :], psG[:, :], ACT.Silu, scale=scale).then_inc(silu, 1)

                def keep(t):
                    a.wait_ge(vt, t + 1)
                    a.activation(vT[:, :, :].rearrange("p c n -> p (c n)"), psW[:, :], ACT.Copy).then_inc(vk, 1)

                silu_of(hback[:, 0:1], 0)
                with a.Fori(0, NT - 1) as t:
                    a.wait_ge(chain, read(t))
                    silu_of(hback[:, ds(t + 1, 1)], t + 1)
                    keep(t)
                keep(NT - 1)

            @block.vector
            def _(v):
                v.wait_ge(wl, 32)
                v.tensor_reduce(ws[:, 0, 0:1], wgv[:, :, :].rearrange("p c n -> p (c n)"), AXX, ALU.add,
                                apply_absolute_value=True).then_inc(wsum, 1)
                v.tensor_reduce(ws[:, 1, 0:1], wo[:, :, :].rearrange("p c n -> p (c n)"), AXX, ALU.add,
                                apply_absolute_value=True).then_inc(wsum, 1)
                v.wait_ge(wmean, 1)
                w = Chain(v, wchain, W_STEPS, 0)
                for n, (wt, tern, size) in enumerate(((wgv, tgv, 2 * 2 * HID), (wo, tos, 8 * D))):
                    w.link(v.tensor_scalar(ws[:, n, 1:2], psM[:, n:n + 1], 1.0 / (size * P), 1e-5, ALU.mult, ALU.max))
                    w.link(v.tensor_scalar(ws[:, n, 2:3], ws[:, n, 1:2], 0.5, None, ALU.mult))
                    w.link(v.tensor_scalar(ws[:, n, 3:4], ws[:, n, 1:2], -0.5, None, ALU.mult))
                    flat = wt[:, :, :].rearrange("p c n -> p (c n)")
                    w.link(v.tensor_scalar(below[:, 0:size], flat, ws[:, n, 3:4], None, ALU.is_lt))
                    w.link(v.scalar_tensor_tensor(out=tern[:, :, :].rearrange("p c n -> p (c n)"), in0=flat,
                                                  scalar=ws[:, n, 2:3], in1=below[:, 0:size], op0=ALU.is_gt,
                                                  op1=ALU.subtract))
                    w.link(v.tensor_scalar(ws[:, n, 0:1], ws[:, n, 1:2], 1.0 / QB, None, ALU.mult))
                assert w.n == W_STEPS
                ln.vector(v)
                v.wait_ge(squares, NT)
                v.tensor_scalar(ss[:, :], ss[:, :], 1.0 / D, EPS, ALU.mult, ALU.add).then_inc(eased, 1)
                v.wait_ge(powd, 1)
                v.wait_ge(nl, 16)
                v.wait_ge(resid, 1)
                for u in range(2):
                    v.wait_ge(ln.normed[u], NT // 2)
                hc = Chain(v, hchain, H_STEPS, 0)
                for t in range(NT):
                    hc.link(v.scalar_tensor_tensor(out=h[:, t, :], in0=xn[:, t, :], scalar=rr[:, t:t + 1],
                                                   in1=nw[:, :], op0=ALU.mult, op1=ALU.mult))
                hc.link(v.tensor_reduce(hmax[:, :], h[:, :, :], AXX, ALU.max, apply_absolute_value=True))
                hc.link(v.tensor_scalar(hmax[:, :], hmax[:, :], 1e-5, None, ALU.max))
                hc.link(v.reciprocal(hinv[:, :], hmax[:, :]))
                hc.link(v.tensor_scalar(hinv[:, :], hinv[:, :], QB, None, ALU.mult))
                hc.link(v.tensor_scalar(hback[:, :], hmax[:, :], ws[:, 0, 0:1], None, ALU.mult))
                for t in range(NT):
                    hc.link(v.tensor_scalar(h[:, t, :], h[:, t, :], hinv[:, t:t + 1], QB, ALU.mult, ALU.min))
                hc.link(v.tensor_scalar(h[:, :, :], h[:, :, :], -QB, MAGIC, ALU.max, ALU.add))
                assert hc.n == H_STEPS
                v.tensor_scalar(hq[:, :, :], h[:, :, :], -MAGIC, None, ALU.add).then_inc(quant, 1)
                v.sem_inc(added, 1)

                def hidden_values(back, keep_back, t):
                    ch = Chain(v, chain, 7, t)
                    v.wait_ge(silu, t + 1)
                    v.wait_ge(vp, t + 1)
                    ch.link(v.scalar_tensor_tensor(out=hv[:, :], in0=psV[:, :], scalar=back, in1=sg[:, :],
                                                   op0=ALU.mult, op1=ALU.mult))
                    ch.link(v.tensor_reduce(am[:, 0:1], hv[:, :], AXX, ALU.max, apply_absolute_value=True))
                    ch.link(v.tensor_scalar(am[:, 0:1], am[:, 0:1], 1e-5, None, ALU.max))
                    ch.link(v.reciprocal(am[:, 1:2], am[:, 0:1]))
                    ch.link(v.tensor_scalar(am[:, 1:2], am[:, 1:2], QB, None, ALU.mult))
                    ch.link(v.tensor_scalar(hr[:, :], hv[:, :], am[:, 1:2], QB, ALU.mult, ALU.min))
                    ch.link(v.tensor_scalar(hr[:, :], hr[:, :], -QB, MAGIC, ALU.max, ALU.add))
                    assert ch.n == 7
                    if not isinstance(t, int):
                        v.wait_ge(vt, t)
                    v.tensor_scalar(vq[:, :], hr[:, :], -MAGIC, None, ALU.add).then_inc(vquant, 1)
                    v.tensor_tensor(keep_back, am[:, 0:1], ws[:, 1, 0:1], ALU.mult).then_inc(backs, 1)

                def add(x, back, t):
                    v.wait_ge(y, t + 1)
                    v.wait_ge(backs, t + 1)
                    v.scalar_tensor_tensor(out=x, in0=psY[:, 0:D].unsqueeze(1), scalar=back, in1=x,
                                           op0=ALU.mult, op1=ALU.add).then_inc(added, 1)

                hidden_values(hback[:, 0:1], vback[:, 0:1], 0)
                with v.Fori(0, NT - 1) as t:
                    hidden_values(hback[:, ds(t + 1, 1)], vback[:, ds(t + 1, 1)], t + 1)
                    add(g.X[:, ds(t, 1), :], vback[:, ds(t, 1)], t)
                add(g.X[:, NT - 1:NT, :], vback[:, NT - 1:NT], NT - 1)


H_STEPS = 2 * NT + 6
W_STEPS = 12


class Globals:
    pass


def setup(nc, g, ins, ctx):
    def sb(name, shape, dt=F32):
        return ctx.enter_context(nc.sbuf_tensor(name, shape, dt))

    g.X = sb("X", [P, NT, D])
    g.xnT = sb("xnT", [P, 2, TOK])
    g.consts = sb("consts", [P, CONST_COLS])
    g.mhalf = sb("mhalf", [P, 16])
    g.ctx32 = sb("ctx32", [DC, TOK])
    g.KVT = sb("KVT", [DC, B, LC])
    g.KVK = sb("KVK", [P, B, 2, DC])
    g.KVL = sb("KVL", [P, B, DC])
    g.ident = g.consts[:, C_IDENT:C_IDENT + P]
    g.hmask16 = g.consts[:, C_HM16:C_HM16 + 8]
    g.hmask2 = g.consts[:, C_HM2:C_HM2 + 32]
    g.vmask = g.consts[:, C_VM:C_VM + 4]
    g.causal = g.consts[:, C_CAUSAL:C_CAUSAL + S]
    g.offdiag = g.consts[:, C_OFFD:C_OFFD + S]
    g.had = g.consts[:, C_HAD:C_HAD + P]
    g.headmean = g.consts[:, C_HMEAN:C_HMEAN + P]
    g.ones = g.consts[:, C_ONES:C_ONES + P]
    g.w = {}
    g.KM = sb("KM", [P, NT, S])
    g.identb = sb("identb", [P, P], BF16)
    g.earlier = sb("earlier", [P, 256])
    with Stage(nc, "load") as st:
        loaded, filled = st.sem("loaded filled")
        n = 0
        jobs = [(g.X[:, :, :], ins["x"].rearrange("(t p) d -> p t d", p=P)), (g.consts[:, :], ins["consts"]),
                (g.ctx32[:, :], ins["ctx32"]), (g.identb[:, :], ins["identb"]), (g.earlier[:, :], ins["earlier"])]
        for name in sorted(WEIGHTS, key=lambda n: n[:2] in LAYER0):
            shape, where = WEIGHTS[name][0], g.layer0 if name[:2] in LAYER0 else ctx
            g.w[name] = where.enter_context(nc.sbuf_tensor("w_" + name, shape, F32))
            jobs.append((g.w[name], ins["w_" + name]))
        with nc.Block() as block:
            @block.sync
            def _(sp):
                for dst, src in jobs:
                    sp.dma_start(dst if isinstance(dst, bass.AP) else dst.ap(), src).then_inc(loaded, 16)
                sp.wait_ge(loaded, 16 * len(jobs))

            @block.vector
            def _(v):
                v.memset(g.mhalf[:, :], -0.5).then_inc(filled, 1)
                v.wait_ge(filled, 1)


def attention_stage(nc, g, name, norm=True, **kw):
    with Stage(nc, name) as st:
        at = Attention(g, st, name, **kw)
        ln = LayerNorm(g, st, [at.psS, at.psT]) if norm else None
        with nc.Block() as block:
            @block.vector
            def _(v):
                if norm:
                    ln.vector(v)
                at.vector(v)

            @block.gpsimd
            def _(p):
                if norm:
                    ln.gpsimd(p)
                    if at.KC > 1:
                        ln.wait(p)
                at.gpsimd(p)

            @block.tensor
            def _(pe):
                if norm:
                    ln.tensor(pe)
                    ln.wait(pe)
                at.tensor(pe)

            @block.scalar
            def _(a):
                if norm:
                    ln.scalar(a)
                at.scalar(a)


def program(nc, ins, out):
    g = Globals()
    with ExitStack() as ctx:
        g.layer0 = ExitStack()
        setup(nc, g, ins, ctx)
        causal = lambda t: g.causal.unsqueeze(1)
        attention_stage(nc, g, "x0", heads=16, hd=16, w={k: g.w["x0" + k] for k in "qkvo"}, kv=g.ctx32,
                        kv_rows=DC, kv_chunks=1, hmask=g.hmask16, mask=causal)
        gated_recurrence_stage(nc, g)
        hadamard_ffn_stage(nc, g, ins["f0stream"], ins["f0row"])
        g.layer0.close()
        context_stage(nc, g, ins)
        with nc.sbuf_tensor("A1", [P, 2, MH * DCQ], F32) as Qm, nc.sbuf_tensor("C1", [HQ, 2, MH * DC], F32) as Cm, \
                nc.sbuf_tensor("D1", [P, 8, D], F32) as Dm:
            fold_stage(nc, g, "w1", ins["x1wide"], ins["x1narrow"], Qm, Cm, Dm)
            latent_stage(nc, g, "x1", Qm, Cm, Dm, g.w["qrope"])
        scratch = nc.dram_tensor("sim_scratch", (NT, 2 * BT, 512), F32).ap()
        similarity_stage(nc, g, scratch)
        attention_stage(nc, g, "a1", norm=False, heads=32, hd=2, w={k: g.w["a1" + k] for k in "qkvo"}, kv=g.xnT,
                        kv_rows=P, kv_chunks=2, hmask=g.hmask2, mask=lambda t: g.KM[:, ds(t, 1), :],
                        bias={k: g.w["a1b" + k] for k in "qkvo"})
        experts_stage(nc, g, "f1", 32, ins["f1stream"], ins["sel1"], 8, g.w["r1"], top_p=0.9)
        attention_stage(nc, g, "x2", heads=16, hd=16, w={k: g.w["x2" + k] for k in "qkvo"}, kv=g.ctx32,
                        kv_rows=DC, kv_chunks=1, hmask=g.hmask16, mask=causal)
        normed_memory_stage(nc, g)
        experts_stage(nc, g, "f2", 25, ins["f2stream"], ins["sel2"], 16, g.w["r2"], top_k=6, shared=True)
        with nc.sbuf_tensor("B3", [P, 2, MH * DC], F32) as Qm, nc.sbuf_tensor("D3", [P, 8, D], F32) as Dm:
            fold_stage(nc, g, "w3", ins["x3wide"], ins["x3narrow"], Qm, None, Dm)
            latent_stage(nc, g, "x3", Qm, None, Dm, None)
        attention_stage(nc, g, "a3", heads=16, hd=16, w={k: g.w["a3" + k] for k in "qkvo"}, kv=g.xnT,
                        kv_rows=P, kv_chunks=2, hmask=g.hmask16, mask=causal, bias={"o": g.w["a3bo"]})
        quantised_ffn_stage(nc, g, ins)
        with Stage(nc, "store") as st:
            stored = st.sem("stored")
            with nc.Block() as block:
                @block.sync
                def _(sp):
                    sp.dma_start(out.rearrange("(t p) d -> p t d", p=P), g.X[:, :, :]).then_inc(stored, 16)
                    sp.wait_ge(stored, 16)


C_IDENT = 0
C_HM16 = C_IDENT + P
C_HM2 = C_HM16 + 8
C_VM = C_HM2 + 32
C_CAUSAL = C_VM + 4
C_OFFD = C_CAUSAL + S
C_HAD = C_OFFD + S
C_HMEAN = C_HAD + P
C_ONES = C_HMEAN + P
CONST_COLS = C_ONES + P


def constants():
    p = np.arange(P)
    c = np.zeros((P, CONST_COLS), np.float32)
    c[:, C_IDENT:C_IDENT + P] = np.eye(P)
    c[:, C_HM16:C_HM16 + 8] = (p[:, None] // 16 == np.arange(8)[None])
    c[:, C_HM2:C_HM2 + 32] = (p[:, None] // 2 == np.arange(32)[None])
    c[:, C_VM:C_VM + 4] = (p[:, None] // S == np.arange(4)[None])
    q, k = p[:, None] % S, np.arange(S)[None]
    c[:, C_CAUSAL:C_CAUSAL + S] = np.where(k <= q, 0.0, NEG)
    c[:, C_OFFD:C_OFFD + S] = (k != q)
    h = np.ones((1, 1))
    while len(h) < P:
        h = np.block([[h, h], [h, -h]])
    c[:, C_HAD:C_HAD + P] = h
    c[:, C_HMEAN:C_HMEAN + P] = (p[:, None] // 64 == p[None] // 64) / 64.0
    c[:, C_ONES:C_ONES + P] = 1.0
    return c


def rows(a, width=P):
    k, n = a.shape
    return np.ascontiguousarray(a.reshape(k // width, width, n).transpose(1, 0, 2))


LAYER0 = ("x0", "a0", "f0")
WEIGHTS = {
    "x0q": ([P, 2, 256], lambda i: rows(i["L0_xattn_Wq"].T)),
    "x0k": ([DC, 1, 256], lambda i: rows(i["L0_xattn_Wkv_expand"][:256].T, DC)),
    "x0v": ([DC, 1, 256], lambda i: rows(i["L0_xattn_Wkv_expand"][256:].T, DC)),
    "x0o": ([P, 2, 256], lambda i: rows(i["L0_xattn_Wout"].T)),
    "a0in": ([P, 2, 256], lambda i: rows(i["L0_attn_W_in"].T)),
    "a0gate": ([P, 2, 256], lambda i: rows(i["L0_attn_W_gate"].T)),
    "a0vec": ([P, 6], lambda i: cols(i["L0_attn_b_in"], i["L0_attn_b_gate"], i["L0_attn_forget_lambda"])),
    "f0down": ([P, 8, 256], lambda i: rows(i["L0_ffn_W_down"].T)),
    "x2q": ([P, 2, 256], lambda i: rows(i["L2_xattn_Wq"].T)),
    "x2k": ([DC, 1, 256], lambda i: rows(i["L2_xattn_Wkv_expand"][:256].T, DC)),
    "x2v": ([DC, 1, 256], lambda i: rows(i["L2_xattn_Wkv_expand"][256:].T, DC)),
    "x2o": ([P, 2, 256], lambda i: rows(i["L2_xattn_Wout"].T)),
    "m2in": ([P, 2, 256], lambda i: rows(i["L2_attn_W_in"].T)),
    "m2gate": ([P, 2, 1024], lambda i: rows(by_gate(i["L2_attn_W_gate"]).T)),
    "m2out": ([P, 2, 256], lambda i: rows(i["L2_attn_W_out"].T)),
    "m2vec": ([P, 9], lambda i: np.concatenate([cols(by_gate(i["L2_attn_b_gate"])),
                                                np.tile(i["L2_attn_rms_w"], 2)[:, None]], axis=1)),
    "r2": ([P, 2, 16], lambda i: rows(i["L2_ffn_gate_w"].T)),
    "a3q": ([P, 2, 256], lambda i: rows(i["L3_attn_Wq"])),
    "a3k": ([P, 2, 256], lambda i: rows(per_head(i["L3_attn_Wk"]))),
    "a3v": ([P, 2, 256], lambda i: rows(per_head(i["L3_attn_Wv"]))),
    "a3o": ([P, 2, 256], lambda i: rows(i["L3_attn_Wo"])),
    "a3bo": ([1, 256], lambda i: i["L3_attn_bo"][None]),
    "s1w1": ([P, 2, P], lambda i: rows(i["L1_attn_W1"].T)),
    "s1w2": ([P, 64], lambda i: i["L1_attn_W2"].T),
    "s1w3": ([P, BT, 2 * BT], lambda i: third_layer(i["L1_attn_W3"])),
    "s1vec": ([P, 7], lambda i: np.concatenate([
        cols(i["L1_attn_gamma"], i["L1_attn_beta"], i["L1_attn_b1"]), np.tile(i["L1_attn_b2"], 2)[:, None],
        np.tile(i["L1_attn_b3"], P)[:, None]], axis=1)),
    "a1q": ([P, 2, 64], lambda i: rows(i["L1_attn_Wqkv"][:64].T)),
    "a1k": ([P, 2, 64], lambda i: rows(i["L1_attn_Wqkv"][64:128].T)),
    "a1v": ([P, 2, 64], lambda i: rows(i["L1_attn_Wqkv"][128:].T)),
    "a1o": ([64, 1, 256], lambda i: rows(i["L1_attn_Wout"].T, 64)),
    "a1bq": ([1, 64], lambda i: i["L1_attn_bqkv"][None, :64]),
    "a1bk": ([1, 64], lambda i: i["L1_attn_bqkv"][None, 64:128]),
    "a1bv": ([1, 64], lambda i: i["L1_attn_bqkv"][None, 128:]),
    "a1bo": ([1, 256], lambda i: i["L1_attn_bout"][None]),
    "r1": ([P, 2, 8], lambda i: rows(i["L1_ffn_router_w"].T)),
    "qrope": ([HQ, 2, 2, S], lambda i: query_rope()),
    "f0vec": ([P, 26], lambda i: cols(i["L0_ffn_SU_ug"], i["L0_ffn_SU_dp"], i["L0_ffn_Wscale_ug"])),
}


def by_gate(w):
    return np.swapaxes(w.reshape(4, 4, 64, -1), 0, 1).reshape(w.shape)


def per_head(w):
    return np.repeat(w.reshape(D, 4, 1, 16), 4, axis=2).reshape(D, D)


def third_layer(w):
    out = np.zeros((P, BT, 2 * BT), np.float32)
    for b in range(BT):
        for ih in range(2):
            out[ih * 64:(ih + 1) * 64, b, 2 * b + ih] = w[0]
    return out


def cols(*vectors):
    return np.concatenate([v.reshape(-1, P).T for v in vectors], axis=1)


def rope_angles(n, dim):
    inv = np.float32(1.0) / np.float32(10000.0) ** (np.arange(0, dim, 2, dtype=np.float32) / np.float32(dim))
    return np.repeat(np.arange(n, dtype=np.float32)[:, None] * inv[None], 2, axis=-1)


def selection(expert_of):
    s = np.zeros((96, len(expert_of)), mybir.dt.np(BF16))
    for k in range(3):
        for n, e in enumerate(expert_of):
            if e >= 0:
                s[32 * k + e, n] = 1
    return s


def query_rope():
    f = rope_angles(S, DCQ).T.reshape(2, HQ, S)
    return np.stack([np.cos(f), np.sin(f)]).transpose(2, 0, 1, 3).astype(np.float32)


def context_arrays(c):
    h = DC // 2
    r = np.concatenate([c[..., h:], c[..., :h]], axis=-1)
    f = rope_angles(LC, DC)
    cos, sin = np.cos(f).astype(np.float32), np.sin(f).astype(np.float32)
    sin[:, :h] *= -1
    out = {}
    for s, x in (("", c), ("r", r)):
        out["kvT" + s] = x.transpose(2, 0, 1)
        out["kvK" + s] = x[:, :2 * P].reshape(B, 2, P, DC).transpose(2, 0, 1, 3)
        out["kvL" + s] = x[:, 2 * P].reshape(-1)
    out["tabT"] = np.stack([cos.T, sin.T], axis=1)
    out["tabK"] = np.stack([cos[:2 * P].reshape(2, P, DC), sin[:2 * P].reshape(2, P, DC)]).transpose(2, 0, 1, 3)
    out["tabL"] = np.concatenate([cos[2 * P], sin[2 * P]])
    return out


def latent_arrays(i, l):
    wq = i[l + "Wq"].reshape(MH, MK, D)
    wo = i[l + "Wo"].T.reshape(MH, MK, D)
    wide = np.concatenate([wq, i[l + "w_kc_q"], i[l + "w_kc_kv"][DOWN_AT], wo[DOWN_AT]], axis=2)
    narrow = np.concatenate([i[l + "W_qr"].transpose(0, 2, 1), i[l + "W_kr"].transpose(0, 2, 1)], axis=2)
    return wide, narrow


def ffn_stream(gate, up, down=None):
    n = -(-gate.shape[0] // P)
    pad = n * P - gate.shape[0]
    parts = []
    for w in (gate, up):
        w = np.pad(w, ((0, pad), (0, 0))).reshape(n, P, 2, P)
        parts.append(w.transpose(0, 3, 2, 1).reshape(n, P, 256))
    if down is not None:
        parts.append(np.pad(down.T, ((0, pad), (0, 0))).reshape(n, P, 256))
    return np.concatenate(parts, axis=2)


def kernel(**inputs):
    import concourse.bacc as _bacc
    from concourse.bass_utils import run_bass_kernel_spmd as _run

    i = {k: np.asarray(v) for k, v in inputs.items()}
    arrays = {
        "x": i["x"].reshape(TOK, D),
        "consts": constants(),
        "identb": np.eye(P).astype(mybir.dt.np(BF16)),
        "earlier": np.broadcast_to(np.arange(16)[None] < np.arange(16)[:, None], (P, 16, 16)).reshape(P, 256).astype(np.float32),
        "sel2": selection(np.where(np.arange(25 * P) < 16 * 176, np.arange(25 * P) // 176, 16)),
        "q3gv": rows(i["L3_ffn_w_gv"].T), "q3out": rows(i["L3_ffn_w_out"].T), "q3norm": i["L3_ffn_norm_w"],
        "sel1": selection(np.arange(32 * P) // 512),
        "ctx32": i["ctx_512"][:, :S, :].reshape(TOK, DC).T,
    }
    arrays |= context_arrays(i["ctx_512"])
    for l in (1, 3):
        arrays[f"x{l}wide"], arrays[f"x{l}narrow"] = latent_arrays(i, f"L{l}_xattn_")
    arrays["f0stream"] = ffn_stream(i["L0_ffn_W_gate"], i["L0_ffn_W_up"])
    arrays["f1stream"] = ffn_stream(i["L1_ffn_gate_w"].reshape(4096, D), i["L1_ffn_up_w"].reshape(4096, D),
                                    i["L1_ffn_down_w"].transpose(1, 0, 2).reshape(D, 4096))
    w13, s13 = i["L2_ffn_w13"], i["L2_ffn_sw13"]
    arrays["f2stream"] = ffn_stream(
        np.concatenate([w13[:, :176].reshape(-1, D), s13[:352]]), np.concatenate([w13[:, 176:].reshape(-1, D), s13[352:]]),
        np.concatenate([i["L2_ffn_w2"].transpose(1, 0, 2).reshape(D, -1), i["L2_ffn_sw2"]], axis=1))
    arrays["f0row"] = i["L0_ffn_Wscale_dp"]
    for name, (shape, lay) in WEIGHTS.items():
        arrays["w_" + name] = lay(i)
    arrays = {k: np.ascontiguousarray(v) for k, v in arrays.items()}
    nc = _bacc.Bacc("TRN2", target_bir_lowering=False, num_devices=1)
    ins = {k: nc.dram_tensor("in_" + k, v.shape, mybir.dt.from_np(v.dtype), kind="ExternalInput").ap()
           for k, v in arrays.items()}
    out = nc.dram_tensor("out_0", (TOK, D), F32, kind="ExternalOutput").ap()
    program(nc, ins, out)
    r = _run(nc, [{"in_" + k: v for k, v in arrays.items()}], core_ids=[0])
    return r.results[0]["out_0"].reshape(B, S, D)
```
